# Optimizing a Trainium2 kernel written in Bass

```python
import numpy as np
import jax
import jax.numpy as jnp

def _softmax(x, axis=-1):
    return jax.nn.softmax(x, axis=axis)

def _gelu(x):
    return jax.nn.gelu(x, approximate=True)

def _silu(x):
    return jax.nn.silu(x)

def _sigmoid(x):
    return jax.nn.sigmoid(x)

def _layernorm(x, axis=-1, eps=1e-05):
    m = jnp.mean(x, axis=axis, keepdims=True)
    v = jnp.var(x, axis=axis, keepdims=True)
    return (x - m) / jnp.sqrt(v + eps)

def _scatter_add(tgt, idx, src, axis=0):
    return tgt.at[idx].add(src)

def _segment_sum(src, seg, n):
    return jax.ops.segment_sum(src, seg, n)
kernel_name = 'mk_gnn_preln_d1_gnn_r64_4df0ab'

def setup_inputs(seed: int=0):
    np.random.seed(seed)
    _w = jnp.asarray

    def _rec_inputs():
        import jax
        import jax.numpy as jnp
        _gk = jax.random.key(seed)
        x = -0.000202 + 1 * jax.random.normal(jax.random.fold_in(_gk, 1), (100000, 128), jnp.float32)
        src = jax.random.randint(jax.random.fold_in(_gk, 2), (25000,), 0, 100000, jnp.int32)
        dst = jax.random.randint(jax.random.fold_in(_gk, 3), (25000,), 0, 100000, jnp.int32)
        _o = jnp.argsort(dst, stable=True)
        src = src[_o]
        dst = dst[_o]
        return (x, src, dst)
    x, src, dst = _rec_inputs()

    def _L0_gnn_setup():
        import jax, jax.numpy as jnp
        import numpy as np
        N = 50000
        E = 12500
        IN_C, HID_C, OUT_C = (128, 256, 128)
        EPS = 1e-05

        def _lin_params(key, out_f, in_f, bias=True):
            kw, kb = jax.random.split(key)
            bound = 1.0 / np.sqrt(in_f)
            W = jax.random.uniform(kw, (out_f, in_f), jnp.float32, -bound, bound)
            if bias:
                b = jax.random.uniform(kb, (out_f,), jnp.float32, -bound, bound)
                return (W, b)
            return (W, None)

        def _mean_agg(x, src, dst, n):
            msg_sum = jax.ops.segment_sum(x[src], dst, num_segments=n)
            cnt = jax.ops.segment_sum(jnp.ones((src.shape[0], 1), x.dtype), dst, num_segments=n)
            return msg_sum / jnp.maximum(cnt, 1.0)

        def _sage_conv(x, src, dst, Wl, bl, Wr):
            agg = _mean_agg(x, src, dst, x.shape[0])
            out = agg @ Wl.T + bl + x @ Wr.T
            return out

        def _batch_norm(x, gamma, beta):
            mu = jnp.mean(x, axis=0)
            var = jnp.mean(jnp.square(x - mu), axis=0)
            return (x - mu) * jax.lax.rsqrt(var + EPS) * gamma + beta
        key = jax.random.key(seed)
        ks = jax.random.split(key, 12)
        x = jax.random.normal(ks[0], (N, IN_C), jnp.float32)
        edge_index = jax.random.randint(ks[1], (2, E), 0, N, dtype=jnp.int64)
        Wl0, bl0 = _lin_params(ks[2], HID_C, IN_C)
        Wr0, _ = _lin_params(ks[3], HID_C, IN_C, bias=False)
        Wl1, bl1 = _lin_params(ks[4], HID_C, HID_C)
        Wr1, _ = _lin_params(ks[5], HID_C, HID_C, bias=False)
        Wl2, bl2 = _lin_params(ks[6], OUT_C, HID_C)
        Wr2, _ = _lin_params(ks[7], OUT_C, HID_C, bias=False)
        gamma0 = jnp.ones((HID_C,), jnp.float32)
        beta0 = jnp.zeros((HID_C,), jnp.float32)
        gamma1 = jnp.ones((HID_C,), jnp.float32)
        beta1 = jnp.zeros((HID_C,), jnp.float32)
        return {'x': x, 'edge_index': edge_index, 'Wl0': Wl0, 'bl0': bl0, 'Wr0': Wr0, 'gamma0': gamma0, 'beta0': beta0, 'Wl1': Wl1, 'bl1': bl1, 'Wr1': Wr1, 'gamma1': gamma1, 'beta1': beta1, 'Wl2': Wl2, 'bl2': bl2, 'Wr2': Wr2}
    _L0_gnn_all = _L0_gnn_setup()
    _L0_gnn_in = {k: v for k, v in _L0_gnn_all.items() if k in ('Wl0', 'bl0', 'Wr0', 'gamma0', 'beta0', 'Wl1', 'bl1', 'Wr1', 'gamma1', 'beta1', 'Wl2', 'bl2', 'Wr2')}
    del _L0_gnn_all
    return {'x': x, 'src': src, 'dst': dst, 'L0_gnn_Wl0': _L0_gnn_in['Wl0'], 'L0_gnn_bl0': _L0_gnn_in['bl0'], 'L0_gnn_Wr0': _L0_gnn_in['Wr0'], 'L0_gnn_gamma0': _L0_gnn_in['gamma0'], 'L0_gnn_beta0': _L0_gnn_in['beta0'], 'L0_gnn_Wl1': _L0_gnn_in['Wl1'], 'L0_gnn_bl1': _L0_gnn_in['bl1'], 'L0_gnn_Wr1': _L0_gnn_in['Wr1'], 'L0_gnn_gamma1': _L0_gnn_in['gamma1'], 'L0_gnn_beta1': _L0_gnn_in['beta1'], 'L0_gnn_Wl2': _L0_gnn_in['Wl2'], 'L0_gnn_bl2': _L0_gnn_in['bl2'], 'L0_gnn_Wr2': _L0_gnn_in['Wr2']}

def reference(x, src, dst, L0_gnn_Wl0, L0_gnn_bl0, L0_gnn_Wr0, L0_gnn_gamma0, L0_gnn_beta0, L0_gnn_Wl1, L0_gnn_bl1, L0_gnn_Wr1, L0_gnn_gamma1, L0_gnn_beta1, L0_gnn_Wl2, L0_gnn_bl2, L0_gnn_Wr2):
    import jax
    import jax.numpy as jnp

    def _L0_gnn_ref(x, edge_index, Wl0, bl0, Wr0, gamma0, beta0, Wl1, bl1, Wr1, gamma1, beta1, Wl2, bl2, Wr2):
        import jax, jax.numpy as jnp
        import numpy as np
        N = 50000
        E = 12500
        IN_C, HID_C, OUT_C = (128, 256, 128)
        EPS = 1e-05

        def _lin_params(key, out_f, in_f, bias=True):
            kw, kb = jax.random.split(key)
            bound = 1.0 / np.sqrt(in_f)
            W = jax.random.uniform(kw, (out_f, in_f), jnp.float32, -bound, bound)
            if bias:
                b = jax.random.uniform(kb, (out_f,), jnp.float32, -bound, bound)
                return (W, b)
            return (W, None)

        def _mean_agg(x, src, dst, n):
            msg_sum = jax.ops.segment_sum(x[src], dst, num_segments=n)
            cnt = jax.ops.segment_sum(jnp.ones((src.shape[0], 1), x.dtype), dst, num_segments=n)
            return msg_sum / jnp.maximum(cnt, 1.0)

        def _sage_conv(x, src, dst, Wl, bl, Wr):
            agg = _mean_agg(x, src, dst, x.shape[0])
            out = agg @ Wl.T + bl + x @ Wr.T
            return out

        def _batch_norm(x, gamma, beta):
            mu = jnp.mean(x, axis=0)
            var = jnp.mean(jnp.square(x - mu), axis=0)
            return (x - mu) * jax.lax.rsqrt(var + EPS) * gamma + beta
        src, dst = (edge_index[0], edge_index[1])
        h = _sage_conv(x, src, dst, Wl0, bl0, Wr0)
        h = jax.nn.relu(_batch_norm(h, gamma0, beta0))
        h = _sage_conv(h, src, dst, Wl1, bl1, Wr1)
        h = jax.nn.relu(_batch_norm(h, gamma1, beta1))
        h = _sage_conv(h, src, dst, Wl2, bl2, Wr2)
        return jax.nn.log_softmax(h, axis=-1)
    edge_index = jnp.stack([src, dst])
    h = jnp.maximum(_layernorm(x, axis=-1), 0.0)
    x = x + _L0_gnn_ref(h, edge_index, L0_gnn_Wl0, L0_gnn_bl0, L0_gnn_Wr0, L0_gnn_gamma0, L0_gnn_beta0, L0_gnn_Wl1, L0_gnn_bl1, L0_gnn_Wr1, L0_gnn_gamma1, L0_gnn_beta1, L0_gnn_Wl2, L0_gnn_bl2, L0_gnn_Wr2)
    return x

_drawn_inputs = setup_inputs


def setup_inputs(seed=0):
    import zlib

    import numpy as np

    out = dict(_drawn_inputs(seed))
    spreads = {'L0_gnn_gamma0': (1.0, 0.6),
     'L0_gnn_beta0': (0.0, 0.8),
     'L0_gnn_gamma1': (1.0, 0.6),
     'L0_gnn_beta1': (0.0, 0.8)}
    factors = {'L0_gnn_bl0': 8.0, 'L0_gnn_bl1': 8.0, 'L0_gnn_bl2': 8.0}
    for name, (base, spread) in spreads.items():
        noise = np.random.default_rng([zlib.crc32(name.encode()), seed]).standard_normal(out[name].shape)
        drawn = base * np.exp(spread * noise) if base else spread * noise
        out[name] = jnp.asarray(drawn.astype(out[name].dtype))
    for name, factor in factors.items():
        out[name] = (out[name] * factor).astype(out[name].dtype)
    return out
```

```python
from contextlib import ExitStack

import concourse.bass as bass
from concourse import mybir

F32 = mybir.dt.float32
I32 = mybir.dt.int32
ALU = mybir.AluOpType
ACT = mybir.ActivationFunctionType
AX_X = mybir.AxisListType.X

P = 128
EPS = 1e-5
PAD_DST = float(1 << 20)


def gnn_kernel(nc, x, src, dst, Wl0, bl0, Wr0, gamma0, beta0, Wl1, bl1, Wr1, gamma1, beta1, Wl2, bl2, Wr2, out):
    N, CIN = x.shape
    E = src.shape[0]
    HID = Wl0.shape[0]
    COUT = Wl2.shape[0]
    NODES = 2 * P
    BLOCKS = -(-N // NODES)
    TAIL_P = (N - (BLOCKS - 1) * NODES) // 2
    ROW = 2 * P
    PAIRS = -(-E // ROW)
    EPAD = PAIRS * ROW
    TILES = 2 * PAIRS
    GROUPS = -(-(BLOCKS + 1) // PAIRS)
    U = 6
    R = 3
    LAST_ROW = E - (PAIRS - 1) * ROW
    assert CIN == P and COUT == P and HID == 2 * P and N % 2 == 0 and PAIRS <= P
    assert GROUPS * PAIRS > BLOCKS

    K_IN = [CIN, HID, HID]
    K_OUT = [HID, HID, COUT]
    CH = [k // P for k in K_IN]

    z_dram = [nc.dram_tensor(f"z{n}", [N, HID], F32, kind="Internal").ap() for n in range(2)]
    y_dram = [nc.dram_tensor(f"y{n}", [EPAD + P, K_OUT[n] + 1], F32, kind="Internal").ap() for n in range(3)]
    dst_rows_dram = nc.dram_tensor("dst_rows", [PAIRS + 1, ROW], F32, kind="Internal").ap()
    start_dram = nc.dram_tensor("starts", [PAIRS, GROUPS], I32, kind="Internal").ap()

    with ExitStack() as ctx:
        def sb(name, shape, dt=F32):
            return ctx.enter_context(nc.sbuf_tensor(name, shape, dt))

        def sem(name):
            return ctx.enter_context(nc.semaphore(name))

        def sems(name, n):
            return [sem(f"{name}{i}") for i in range(n)]

        ps_t = [ctx.enter_context(nc.psum_tensor(f"ps_t{i}", [P, 512], F32)) for i in range(R)]
        ps_z = [ctx.enter_context(nc.psum_tensor(f"ps_z{i}", [P, 512], F32)) for i in range(R)]
        ps_m = [ctx.enter_context(nc.psum_tensor(f"ps_m{i}", [P, 512], F32)) for i in range(2)]

        ident = sb("ident", [P, P])
        ones = sb("ones", [P, P])
        node_of_col = sb("node_of_col", [P, 2, P])
        neg_dummy = sb("eps_col", [P, 1])
        block_base = sb("block_base", [P, BLOCKS])
        w_raw = sb("w_raw", [P, 6, 2, HID])
        wT = sb("wT", [P, 6, 2, HID])
        cols_in = sb("cols_in", [P, 6, 2])
        bias2 = sb("bias2", [P, 2, COUT])
        scale_c = sb("scale_c", [P, 2, 2])
        shift_c = sb("shift_c", [P, 2, 2])
        bn_tmp = sb("bn_tmp", [P, 10, 2])

        src_i = sb("src_i", [P, ROW], I32)
        dst_i = sb("dst_i", [P, ROW], I32)
        src_f = sb("src_f", [P, ROW])
        dst_f = sb("dst_f", [P, ROW])
        dst_prev = sb("dst_prev", [P, ROW])
        dst_next = sb("dst_next", [P, ROW])
        edge_no = sb("edge_no", [P, ROW])
        run_a = sb("run_a", [P, ROW])
        run_b = sb("run_b", [P, ROW])
        run_first = sb("run_first", [P, ROW])
        run_last = sb("run_last", [P, ROW])
        inv_cnt = sb("inv_cnt", [P, ROW])
        row_ends = sb("row_ends", [P, 2])
        row_line = sb("row_line", [1, 4, P])
        carry = sb("carry", [P, 2])
        diag = sb("diag", [P, P])
        thresholds = sb("thresholds", [P, GROUPS])
        coarse = sb("coarse", [P, GROUPS])
        coarse_i = sb("coarse_i", [P, GROUPS], I32)
        found_row = sb("found_row", [P, GROUPS, ROW])
        fine = sb("fine", [P, GROUPS])
        scratch = sb("scratch", [P, ROW])
        start_i = sb("start_i", [P, GROUPS], I32)
        start_line = sb("start_line", [1, PAIRS * GROUPS], I32)
        src_col = sb("src_col", [P, TILES], I32)
        dst_col = sb("dst_col", [P, TILES])
        inv_col = sb("inv_col", [P, TILES])
        idx_ring = sb("idx_ring", [P, U, 2], I32)
        y_pad = sb("y_pad", [P, HID + 1])

        rows_in = sb("rows_in", [P, U, 2, HID])
        x_in = sb("x_in", [P, U, 2, CIN])
        win = sb("win", [P, U, HID + 1])
        ln_stats = sb("ln_stats", [P, U, 2, 6])
        ln_mv = sb("ln_mv", [P, U, 2, 2])
        ln_std = sb("ln_std", [P, U, 2])
        ln_rstd = sb("ln_rstd", [P, U, 2])
        ln_shift = sb("ln_shift", [P, U, 2])
        h_rows = sb("h_rows", [P, R, 2, CIN])
        hT = sb("hT", [P, R, 2, 2, P])
        sel = sb("sel", [P, R, 2, P])
        z_sb = sb("z_sb", [P, R, 512])
        z_sq = sb("z_sq", [P, R, 512])
        y_sb = sb("y_sb", [P, R, 2, HID + 1])
        acc_z = sb("acc_z", [P, 512])
        acc_sq = sb("acc_sq", [P, 512])
        t_sb = sb("t_sb", [P, R, 2, COUT])
        e_sb = sb("e_sb", [P, R, 2, COUT])
        neg_max = sb("neg_max", [P, R, 2])
        exp_sum = sb("exp_sum", [P, R, 2])
        log_sum = sb("log_sum", [P, R, 2])
        soft_shift = sb("soft_shift", [P, R, 2])
        out_sb = sb("out_sb", [P, R, 2, COUT])

        s_const = sem("s_const")
        s_params = sem("s_params")
        s_pool = sem("s_pool")
        s_wt = sem("s_wt")
        s_wc = sem("s_wc")
        s_edges = sem("s_edges")
        s_dstf = sem("s_dstf")
        s_shift = sem("s_shift")
        s_meta = sem("s_meta")
        s_meta_pe = sem("s_meta_pe")
        s_found = sem("s_found")
        s_start = sem("s_start")
        s_ypad = sem("s_ypad")
        s_bn_pe = sem("s_bn_pe")
        s_bn = sem("s_bn")
        s_bn_sqrt = sem("s_bn_sqrt")
        s_bn_ready = sem("s_bn_ready")

        class Ring:
            pass

        edge, node = [], []
        for l in range(3):
            for kind, into in (("e", edge), ("n", node)):
                r = Ring()
                r.loaded = sems(f"{kind}{l}_loaded", U)
                r.turned = sem(f"{kind}{l}_turned")
                r.hT = sem(f"{kind}{l}_hT")
                r.prod = sem(f"{kind}{l}_prod")
                r.out = sem(f"{kind}{l}_out")
                r.stored = sems(f"{kind}{l}_stored", R)
                if l == 0:
                    r.stat = sem(f"{kind}{l}_stat")
                    r.std = sem(f"{kind}{l}_std")
                    r.rstd = sem(f"{kind}{l}_rstd")
                    r.rows = sem(f"{kind}{l}_rows")
                if kind == "e":
                    r.idx = sem(f"e{l}_idx")
                else:
                    r.sel = sem(f"n{l}_sel")
                    if l < 2:
                        r.acc = sem(f"n{l}_acc")
                    else:
                        r.top = sem("n2_top")
                        r.log = sem("n2_log")
                into.append(r)
        s_chain = sem("s_chain")

        s_ln = {k: sem(f"s_ln_{k}") for k in "en"}
        s_rec = {k: sem(f"s_rec_{k}") for k in "en"}
        s_gate = sem("s_gate")
        s_gate_pool = sem("s_gate_pool")
        s_exp = sem("s_exp")
        s_logit = sem("s_logit")
        s_shift2 = sem("s_shift2")
        for l in range(2):
            node[l].sq = sem(f"n{l}_sq")

        META_COARSE = 17
        META_INV = 24
        META_COLS = 25
        META_START = 26
        LOADS = {"e": [32, 32, 32], "n": [32, 32, 48]}

        def uses(blocks, slot, slots):
            return (blocks - slot + slots - 1) // slots

        def pipeline(eng, count, stages):
            most = max(o for o, _ in stages)
            full = (count - 1 - most) // U

            def step(i):
                for o, stage in stages:
                    if 0 <= i + o < count:
                        stage(i + o)

            for i in range(-most, U):
                step(i)
            with eng.Fori(1, full) as k:
                for r in range(U):
                    for o, stage in stages:
                        stage((r + o) + k * U, slot=(r + o) % U, turn=k + (r + o) // U)
            for i in range(full * U, count):
                step(i)

        def item(fn):
            def stage(i, slot=None, turn=None):
                if slot is None:
                    slot, turn = i % U, i // U
                fn(i, slot, turn, slot % R, turn * (U // R) + slot // R)
            return stage

        def free(eng, s, value):
            if isinstance(value, int) and value <= 0:
                return
            eng.wait_ge(s, value)

        def after(eng, s, i, lag):
            if isinstance(i, int):
                if i >= lag:
                    eng.wait_ge(s, i - lag + 1)
                return
            eng.wait_ge(s, i + (1 - lag))

        block = ctx.enter_context(nc.Block())

        def filled(i):
            return TAIL_P if isinstance(i, int) and i == BLOCKS - 1 else P

        W_ALL = [Wl0, Wr0, Wl1, Wr1, Wl2, Wr2]

        def y_rows(l, i):
            return y_dram[l][bass.ds(i * ROW, ROW), :].rearrange("(a p) f -> p a f", a=2)

        def node_rows(a, i, n):
            return a[bass.ds(i * NODES, 2 * n), :].rearrange("(p j) f -> p j f", j=2)

        @block.sync
        def _(sp):
            sp.wait_ge(s_const, 2)
            for a, t in ((src, src_i), (dst, dst_i)):
                sp.dma_start(t[0:PAIRS - 1, :], a[0:(PAIRS - 1) * ROW].rearrange("(r c) -> r c", c=ROW)).then_inc(s_edges, 16)
                sp.dma_start(t[PAIRS - 1:PAIRS, 0:LAST_ROW], a[(PAIRS - 1) * ROW:E].rearrange("(r c) -> r c", r=1)).then_inc(s_edges, 16)
            for m, w in enumerate(W_ALL):
                o, k = w.shape
                sp.dma_start(w_raw[:, m, 0:o // P, 0:k], w.rearrange("(c p) k -> p c k", p=P)).then_inc(s_params, 16)
            with nc.allow_non_contiguous_dma(reason="a few hundred values"):
                for m, v in enumerate((gamma0, beta0, bl0, gamma1, beta1, bl1)):
                    sp.dma_start(cols_in[:, m, :], v.rearrange("(c p) -> p c", p=P)).then_inc(s_params, 16)
            for j in range(2):
                sp.dma_start(bias2[:, j, :], bl2.rearrange("(a f) -> a f", a=1).to_broadcast([P, COUT])).then_inc(s_params, 16)
            sp.wait_ge(s_meta, 2)
            sp.dma_start(dst_rows_dram[0:PAIRS, :], dst_f[0:PAIRS, :]).then_inc(s_dstf, 16)
            sp.wait_ge(s_const, 5)
            sp.dma_start(dst_rows_dram[PAIRS:PAIRS + 1, :], scratch[0:1, :]).then_inc(s_dstf, 16)
            sp.wait_ge(s_dstf, 32)
            flat = dst_rows_dram.rearrange("r c -> (r c)")
            sp.dma_start(dst_prev[1:PAIRS, :], flat[ROW - 1:EPAD - 1].rearrange("(r c) -> r c", c=ROW)).then_inc(s_shift, 16)
            sp.dma_start(dst_prev[0:1, 1:ROW], flat[0:ROW - 1].rearrange("(r c) -> r c", r=1)).then_inc(s_shift, 16)
            sp.dma_start(dst_next[0:PAIRS, :], flat[1:EPAD + 1].rearrange("(r c) -> r c", c=ROW)).then_inc(s_shift, 16)
            sp.wait_ge(s_const, 4)
            for l in range(3):
                sp.dma_start(y_dram[l][EPAD:EPAD + P, :], y_pad[:, HID - K_OUT[l]:HID + 1]).then_inc(s_ypad, 16)
            sp.wait_ge(s_meta, META_START)
            sp.dma_start(start_dram, start_i[0:PAIRS, :]).then_inc(s_start, 16)
            sp.wait_ge(s_start, 16)
            sp.dma_start(start_line[0:1, :], start_dram.rearrange("r g -> (r g)").rearrange("(a n) -> a n", a=1)).then_inc(s_start, 16)
            sp.wait_ge(s_start, 32)
            sp.wait_ge(s_ypad, 48)

            for l in range(3):
                e, n = edge[l], node[l]
                W = K_OUT[l]

                def store_messages(i, u, t, v, w):
                    sp.wait_ge(e.out, i + 1)
                    sp.dma_start(y_rows(l, i), y_sb[:, v, :, 0:W + 1]).then_inc(e.stored[v], 16)

                pipeline(sp, PAIRS, [(0, item(store_messages))])
                for v in range(R):
                    sp.wait_ge(e.stored[v], 16 * uses(PAIRS, v, R))

                def load_block(i, u, t, v, w):
                    q = filled(i)
                    if l == 0:
                        after(sp, n.rows, i, U)
                    else:
                        after(sp, n.turned, i, U)
                    after(sp, n.prod, i, U)
                    a = x if l == 0 else z_dram[l - 1]
                    sp.dma_start(rows_in[0:q, u, :, 0:K_IN[l]], node_rows(a, i, q)).then_inc(n.loaded[u], 16)
                    start = sp.value_load(start_line[0:1, bass.ds(i, 1)], min_val=0, max_val=EPAD)
                    sp.dma_start(win[:, u, 0:W + 1], y_dram[l][bass.ds(start, P), :]).then_inc(n.loaded[u], 16)
                    if l == 2:
                        after(sp, n.out, i, U)
                        sp.dma_start(x_in[0:q, u, :, :], node_rows(x, i, q)).then_inc(n.loaded[u], 16)

                def store_block(i, u, t, v, w):
                    q = filled(i)
                    sp.wait_ge(n.out, i + 1)
                    if l < 2:
                        sp.dma_start(node_rows(z_dram[l], i, q), z_sb[0:q, v, :].rearrange("p (j f) -> p j f", j=2)).then_inc(n.stored[v], 16)
                    else:
                        sp.dma_start(node_rows(out, i, q), out_sb[0:q, v, :, :]).then_inc(n.stored[v], 16)

                pipeline(sp, BLOCKS, [(U - 1, item(load_block)), (0, item(store_block))])
                for v in range(R):
                    sp.wait_ge(n.stored[v], 16 * uses(BLOCKS, v, R))


        @block.gpsimd
        def _(pool):
            pool.memset(src_i[:, :], 0).then_inc(s_const, 1)
            pool.memset(dst_i[:, :], int(PAD_DST)).then_inc(s_const, 1)
            pool.memset(scratch[:, :], PAD_DST).then_inc(s_const, 1)
            pool.memset(y_pad[:, :], -1.0).then_inc(s_const, 1)
            pool.memset(dst_prev[:, :], -1.0).then_inc(s_const, 1)
            pool.memset(ident[:, :], 0.0).then_inc(s_pool, 1)
            pool.memset(ones[:, :], 1.0).then_inc(s_const, 1)
            pool.wait_ge(s_pool, 1)
            pool.affine_select(out=ident[:, :], in_=ident[:, :], compare_op=ALU.not_equal, fill=1.0,
                               base=0, pattern=[[-1, P]], channel_multiplier=1).then_inc(s_const, 1)
            pool.iota(edge_no[:, :], pattern=[[1, ROW]], base=0, channel_multiplier=ROW,
                      allow_small_or_imprecise_dtypes=True).then_inc(s_const, 1)
            pool.iota(thresholds[:, :], pattern=[[NODES, GROUPS]], base=0, channel_multiplier=GROUPS * NODES,
                      allow_small_or_imprecise_dtypes=True).then_inc(s_const, 1)
            pool.iota(node_of_col[:, :, :], pattern=[[1, 2], [2, P]], base=0, channel_multiplier=0,
                      allow_small_or_imprecise_dtypes=True).then_inc(s_const, 1)
            pool.iota(block_base[:, :], pattern=[[NODES, BLOCKS]], base=0, channel_multiplier=0,
                      allow_small_or_imprecise_dtypes=True).then_inc(s_const, 1)
            pool.memset(neg_dummy[:, :], EPS).then_inc(s_const, 1)
            pool.wait_ge(s_meta, META_COARSE)
            pool.wait_ge(s_dstf, 32)
            for g in range(GROUPS):
                pool.indirect_dma_start(out=found_row[0:PAIRS, g, :], out_offset=None, in_=dst_rows_dram,
                                        in_offset=bass.IndirectOffsetOnAxis(ap=coarse_i[0:PAIRS, g:g + 1], axis=0),
                                        bounds_check=PAIRS, oob_is_err=False).then_inc(s_found, 16)
            pool.wait_ge(s_meta, META_COLS)
            for l in range(3):
                e = edge[l]
                if l > 0:
                    for v in range(R):
                        pool.wait_ge(node[l - 1].stored[v], 16 * uses(BLOCKS, v, R))
                source = x if l == 0 else z_dram[l - 1]

                def gather(i, u, t, v, w):
                    after(pool, e.rows if l == 0 else e.turned, i, U)
                    pool.sem_inc(s_gate_pool, 1)
                    pool.tensor_copy(idx_ring[:, u, :], src_col[:, bass.ds(i * 2, 2)]).then_inc(e.idx, 1)
                    pool.wait_ge(e.idx, i + 1)
                    pool.sem_inc(s_gate_pool, 1)
                    for a in range(2):
                        pool.indirect_dma_start(out=rows_in[:, u, a, 0:K_IN[l]], out_offset=None, in_=source,
                                                in_offset=bass.IndirectOffsetOnAxis(ap=idx_ring[:, u, a:a + 1], axis=0),
                                                bounds_check=N - 1, oob_is_err=False).then_inc(e.loaded[u], 16)

                pipeline(pool, PAIRS, [(0, item(gather))])


        @block.tensor
        def _(pe):
            pe.wait_ge(s_const, 12)
            pe.wait_ge(s_meta, 9)
            for c in range(2):
                mm = pe.transpose(ps_m[0][0:1, c * P:c * P + PAIRS], row_ends[0:PAIRS, c:c + 1], ident[0:PAIRS, 0:PAIRS])
            mm.then_inc(s_meta_pe, 1)
            pe.wait_ge(s_meta, 10)
            pe.matmul(ps_m[1][0:PAIRS, 0:PAIRS], ones[0:PAIRS, 0:PAIRS], diag[0:PAIRS, 0:PAIRS],
                      start=True, stop=True).then_inc(s_meta_pe, 1)
            pe.wait_ge(s_meta, 14)
            for c in range(2):
                mm = pe.transpose(ps_m[0][0:PAIRS, 256 + c:257 + c], row_line[0:1, 2 + c, 0:PAIRS], ident[0:1, 0:1])
            mm.then_inc(s_meta_pe, 1)
            pe.wait_ge(s_meta, META_INV)
            for c, t in enumerate((src_f, dst_f, inv_cnt)):
                for a in range(2):
                    mm = pe.transpose(ps_t[c][:, a * P:a * P + PAIRS], t[0:PAIRS, a * P:(a + 1) * P], ident[0:PAIRS, 0:PAIRS])
            mm.then_inc(s_meta_pe, 1)
            pe.wait_ge(s_params, 16 * 14)
            g = 0
            for m, w in enumerate(W_ALL):
                o, k = w.shape
                for c in range(k // P):
                    if g >= R:
                        pe.wait_ge(s_wc, g - R + 1)
                    for h in range(o // P):
                        mm = pe.transpose(ps_z[g % R][:, h * P:(h + 1) * P], w_raw[:, m, h, c * P:(c + 1) * P], ident[:, :])
                    mm.then_inc(s_wt, 1)
                    g += 1
            pe.wait_ge(s_wc, g)
            pe.wait_ge(s_meta, META_COLS)

            for l in range(3):
                W = K_OUT[l]

                def stages(r, kind):
                    def turn(i, u, t, v, w):
                        q = filled(i) if kind == "n" else P
                        if l == 0:
                            pe.wait_ge(r.rows, i + 1)
                        else:
                            pe.wait_ge(r.loaded[u], (t + 1) * LOADS[kind][l])
                        after(pe, r.hT, i, R)
                        for c in range(CH[l]):
                            for j in range(2):
                                a = h_rows[0:q, v, j, :] if l == 0 else rows_in[0:q, u, j, c * P:(c + 1) * P]
                                mm = pe.transpose(ps_t[v][:, (2 * c + j) * P:(2 * c + j) * P + q], a, ident[0:q, 0:q])
                        mm.then_inc(r.turned, 1)

                    def product(i, u, t, v, w):
                        q = filled(i) if kind == "n" else P
                        if kind == "n":
                            pe.wait_ge(r.sel, i + 1)
                            pe.wait_ge(r.loaded[u], (t + 1) * LOADS[kind][l])
                        after(pe, r.out if kind == "e" else (r.sq if l < 2 else r.top), i, R)
                        if kind == "n":
                            for j in range(2):
                                pe.matmul(ps_z[v][0:q, j * W:(j + 1) * W], sel[:, v, j, 0:q], win[:, u, 0:W],
                                          start=(j == 0), stop=False, skip_group_check=True)
                        pe.wait_ge(r.hT, i + 1)
                        for j in range(2):
                            for c in range(CH[l]):
                                mm = pe.matmul(ps_z[v][0:q, j * W:(j + 1) * W], hT[:, v, c, j, 0:q],
                                               wT[:, 2 * l + (kind == "n"), c, 0:W],
                                               start=(kind == "e" and j == 0 and c == 0), stop=(j == 1 and c == CH[l] - 1),
                                               skip_group_check=True)
                        mm.then_inc(r.prod, 1)

                    return [(1, item(turn)), (0, item(product))]

                pipeline(pe, PAIRS, stages(edge[l], "e"))
                pipeline(pe, BLOCKS, stages(node[l], "n"))
                if l < 2:
                    pe.wait_ge(node[l].acc, BLOCKS)
                    for s, acc in enumerate((acc_z, acc_sq)):
                        for c in range(2):
                            for j in range(2):
                                mm = pe.matmul(ps_m[0][:, 2 * s + c:2 * s + c + 1], acc[:, j * W + c * P:j * W + (c + 1) * P],
                                               ones[:, 0:1], start=(j == 0), stop=(j == 1), skip_group_check=True)
                    mm.then_inc(s_bn_pe, 1)


        @block.scalar
        def _(act):
            g = 0
            for m, w in enumerate(W_ALL):
                o, k = w.shape
                for c in range(k // P):
                    act.wait_ge(s_wt, g + 1)
                    act.activation(wT[:, m, c, 0:o], ps_z[g % R][:, 0:o], ACT.Copy).then_inc(s_wc, 1)
                    g += 1
            act.wait_ge(s_const, 12)

            for l in range(3):
                W = K_OUT[l]
                if l > 0:
                    act.wait_ge(s_bn_ready, l)
                act.preload_act_table_set("sqrt_and_others" if l < 2 else "natural_log_exp_and_others")

                def stages(r, kind):
                    def std(i, u, t, v, w):
                        q = filled(i) if kind == "n" else P
                        act.wait_ge(r.stat, i + 1)
                        after(act, r.rstd, i, U)
                        act.activation(ln_std[0:q, u, :], ln_mv[0:q, u, :, 1], ACT.Sqrt, bias=neg_dummy[0:q, :]).then_inc(r.std, 1)

                    def norm(i, u, t, v, w):
                        q = filled(i) if kind == "n" else P
                        act.wait_ge(r.rstd, i + 1)
                        act.wait_ge(r.loaded[u], (t + 1) * LOADS[kind][0])
                        after(act, r.turned, i, R)
                        for j in range(2):
                            ins = act.activation(h_rows[0:q, v, j, :], rows_in[0:q, u, j, 0:CIN], ACT.Relu,
                                                 bias=ln_shift[0:q, u, j:j + 1], scale=ln_rstd[0:q, u, j:j + 1])
                        ins.then_inc(r.rows, 1)

                    def copy_hT(i, u, t, v, w):
                        q = filled(i) if kind == "n" else P
                        act.wait_ge(r.turned, i + 1)
                        after(act, r.prod, i, R)
                        for c in range(CH[l]):
                            a = ps_t[v][:, 2 * c * P:2 * (c + 1) * P].rearrange("p (j n) -> p j n", j=2)[:, :, 0:q]
                            if l == 0:
                                ins = act.activation(hT[:, v, c, :, 0:q], a, ACT.Copy)
                            else:
                                ins = act.activation(hT[:, v, c, :, 0:q], a, ACT.Relu,
                                                     bias=shift_c[:, l - 1, c:c + 1], scale=scale_c[:, l - 1, c:c + 1])
                        ins.then_inc(r.hT, 1)

                    def copy_z(i, u, t, v, w):
                        q = filled(i)
                        act.wait_ge(r.prod, i + 1)
                        free(act, r.stored[v], w * 16)
                        after(act, r.acc, i, R)
                        act.activation(z_sb[0:q, v, :], ps_z[v][0:q, :], ACT.Copy).then_inc(r.out, 1)
                        act.activation(z_sq[0:q, v, :], ps_z[v][0:q, :], ACT.Square).then_inc(r.sq, 1)

                    def soft(i, u, t, v, w):
                        q = filled(i)
                        act.wait_ge(r.top, i + 1)
                        for j in range(2):
                            ins = act.activation(e_sb[0:q, v, j, :], t_sb[0:q, v, j, :], ACT.Exp,
                                                 bias=neg_max[0:q, v, j:j + 1], accum_out=exp_sum[0:q, v, j:j + 1])
                        ins.then_inc(s_exp, 1)
                        act.wait_ge(s_exp, i + 1)
                        after(act, r.out, i, R)
                        act.activation(log_sum[0:q, v, :], exp_sum[0:q, v, :], ACT.Ln).then_inc(r.log, 1)

                    first = [(3, item(std)), (2, item(norm))] if l == 0 else []
                    last = [] if kind == "e" else [(0, item(copy_z if l < 2 else soft))]
                    return first + [(1, item(copy_hT))] + last

                pipeline(act, PAIRS, stages(edge[l], "e"))
                pipeline(act, BLOCKS, stages(node[l], "n"))
                if l < 2:
                    act.wait_ge(s_bn, 6 * (l + 1) + 6 * l)
                    act.activation(bn_tmp[:, 5, :], bn_tmp[:, 4, :], ACT.Sqrt, bias=neg_dummy[:, :]).then_inc(s_bn_sqrt, 1)


        @block.vector
        def _(dve):
            done = [0]

            def link(ins):
                ins.then_inc(s_meta, 1)
                done[0] += 1
                dve.wait_ge(s_meta, done[0])

            R_ = slice(0, PAIRS)
            dve.wait_ge(s_edges, 64)
            link(dve.tensor_copy(src_f[:, :], src_i[:, :]))
            link(dve.tensor_copy(dst_f[:, :], dst_i[:, :]))
            dve.wait_ge(s_const, 12)
            dve.wait_ge(s_shift, 48)
            link(dve.tensor_tensor(run_a[R_, :], dst_f[R_, :], dst_prev[R_, :], ALU.not_equal))
            link(dve.tensor_tensor(run_a[R_, :], run_a[R_, :], edge_no[R_, :], ALU.mult))
            link(dve.tensor_tensor(run_b[R_, :], dst_f[R_, :], dst_next[R_, :], ALU.is_equal))
            link(dve.scalar_tensor_tensor(out=run_b[R_, :], in0=run_b[R_, :], scalar=PAD_DST, in1=edge_no[R_, :],
                                          op0=ALU.mult, op1=ALU.add))
            link(dve.tensor_tensor_scan(run_first[R_, :], run_a[R_, :], run_a[R_, :], 0.0, ALU.max, ALU.max))
            link(dve.tensor_tensor_scan(run_last[R_, ::-1], run_b[R_, ::-1], run_b[R_, ::-1], 4 * PAD_DST, ALU.min, ALU.min))
            link(dve.tensor_copy(row_ends[R_, 0:1], run_first[R_, ROW - 1:ROW])) if False else None
            dve.tensor_copy(row_ends[R_, 0:1], run_first[R_, ROW - 1:ROW])
            link(dve.tensor_copy(row_ends[R_, 1:2], run_last[R_, 0:1]))
            link(dve.tensor_scalar(diag[R_, R_], ident[R_, R_], dst_f[R_, ROW - 1:ROW], None, ALU.mult))
            dve.wait_ge(s_meta_pe, 1)
            link(dve.tensor_copy(row_line[0:1, 0:2, R_], ps_m[0][0:1, 0:2 * P].rearrange("p (c n) -> p c n", c=2)[:, :, R_]))
            link(dve.memset(row_line[0:1, 2, 0:1], 0.0))
            dve.memset(row_line[0:1, 3, PAIRS - 1:PAIRS], 4 * PAD_DST)
            link(dve.tensor_tensor_scan(row_line[0:1, 2, 1:PAIRS], row_line[0:1, 0, 0:PAIRS - 1], row_line[0:1, 0, 0:PAIRS - 1],
                                        0.0, ALU.max, ALU.max))
            link(dve.tensor_tensor_scan(row_line[0:1, 3, PAIRS - 2::-1], row_line[0:1, 1, PAIRS - 1:0:-1],
                                        row_line[0:1, 1, PAIRS - 1:0:-1], 4 * PAD_DST, ALU.min, ALU.min))
            dve.wait_ge(s_meta_pe, 2)
            link(dve.tensor_copy(diag[R_, R_], ps_m[1][R_, R_]))
            for g in range(GROUPS):
                ins = dve.tensor_scalar(scratch[R_, R_], diag[R_, R_], thresholds[R_, g:g + 1], None, ALU.is_lt, ALU.add,
                                        accum_out=coarse[R_, g:g + 1])
                if g < GROUPS - 1:
                    ins.then_inc(s_chain, 1)
                    dve.wait_ge(s_chain, g + 1)
            link(ins)
            link(dve.tensor_copy(coarse_i[R_, :], coarse[R_, :]))
            dve.wait_ge(s_meta_pe, 3)
            link(dve.tensor_copy(carry[R_, :], ps_m[0][R_, 256:258]))
            link(dve.tensor_scalar(run_first[R_, :], run_first[R_, :], carry[R_, 0:1], None, ALU.max))
            link(dve.tensor_scalar(run_last[R_, :], run_last[R_, :], carry[R_, 1:2], None, ALU.min))
            link(dve.tensor_tensor(run_a[R_, :], run_last[R_, :], run_first[R_, :], ALU.subtract))
            link(dve.tensor_scalar(run_b[R_, :], run_a[R_, :], 1.0, 1.0, ALU.add, ALU.max))
            link(dve.reciprocal(inv_cnt[R_, :], run_b[R_, :]))
            link(dve.memset(acc_z[:, :], 0.0))
            dve.wait_ge(s_meta_pe, 4)
            for c, t in enumerate((src_col, dst_col, inv_col)):
                ins = dve.tensor_copy(t[:, :].rearrange("p (r a) -> p a r", a=2),
                                      ps_t[c][:, 0:2 * P].rearrange("p (a r) -> p a r", a=2)[:, :, R_])
            link(ins)
            dve.wait_ge(s_found, 16 * GROUPS)
            for g in range(GROUPS):
                dve.tensor_scalar(scratch[R_, :], found_row[R_, g, :], thresholds[R_, g:g + 1], None, ALU.is_lt, ALU.add,
                                  accum_out=fine[R_, g:g + 1]).then_inc(s_chain, 1)
                dve.wait_ge(s_chain, GROUPS + g)
            dve.scalar_tensor_tensor(out=start_i[R_, :], in0=coarse[R_, :], scalar=float(ROW), in1=fine[R_, :],
                                     op0=ALU.mult, op1=ALU.add).then_inc(s_meta, 1)
            dve.memset(acc_sq[:, :], 0.0).then_inc(s_meta, 1)
            dve.wait_ge(s_meta, 27)

            for l in range(3):
                W = K_OUT[l]

                def stages(r, kind):
                    def stat(i, u, t, v, w):
                        q = filled(i) if kind == "n" else P
                        dve.wait_ge(r.loaded[u], (t + 1) * LOADS[kind][0])
                        for j in range(2):
                            dve.bn_stats(ln_stats[0:q, u, j, :], rows_in[0:q, u, j, 0:CIN]).then_inc(s_ln[kind], 1)
                        after(dve, r.std, i, U)
                        dve.wait_ge(s_ln[kind], i * 2 + 2)
                        dve.sem_inc(s_gate, 1)
                        for j in range(2):
                            ins = dve.bn_aggr(ln_mv[0:q, u, j, :], ln_stats[0:q, u, j, :])
                        ins.then_inc(r.stat, 1)

                    def rstd(i, u, t, v, w):
                        q = filled(i) if kind == "n" else P
                        dve.wait_ge(r.std, i + 1)
                        after(dve, r.rows, i, U)
                        dve.reciprocal(ln_rstd[0:q, u, :], ln_std[0:q, u, :]).then_inc(s_rec[kind], 1)
                        dve.wait_ge(s_rec[kind], i + 1)
                        dve.scalar_tensor_tensor(out=ln_shift[0:q, u, :], in0=ln_mv[0:q, u, :, 0], scalar=-1.0,
                                                 in1=ln_rstd[0:q, u, :], op0=ALU.mult, op1=ALU.mult).then_inc(r.rstd, 1)

                    def messages(i, u, t, v, w):
                        dve.wait_ge(r.prod, i + 1)
                        free(dve, r.stored[v], w * 16)
                        dve.tensor_copy(y_sb[:, v, :, W:W + 1], dst_col[:, bass.ds(i * 2, 2)].rearrange("p (a o) -> p a o", o=1))
                        for a in range(2):
                            ins = dve.tensor_scalar(y_sb[:, v, a, 0:W], ps_z[v][:, a * W:(a + 1) * W],
                                                    inv_col[:, bass.ds(i * 2 + a, 1)], None, ALU.mult)
                        ins.then_inc(r.out, 1)

                    def select(i, u, t, v, w):
                        dve.wait_ge(r.loaded[u], (t + 1) * LOADS[kind][l])
                        after(dve, r.prod, i, R)
                        dve.tensor_scalar(sel[:, v, :, :], node_of_col[:, :, :], block_base[:, bass.ds(i, 1)],
                                          win[:, u, W:W + 1], ALU.add, ALU.is_equal).then_inc(r.sel, 1)

                    def sums(i, u, t, v, w):
                        q = filled(i)
                        dve.wait_ge(r.sq, i + 1)
                        dve.wait_ge(r.out, i + 1)
                        after(dve, r.acc, i, 1)
                        dve.tensor_tensor(acc_z[0:q, :], acc_z[0:q, :], z_sb[0:q, v, :], ALU.add)
                        dve.tensor_tensor(acc_sq[0:q, :], acc_sq[0:q, :], z_sq[0:q, v, :], ALU.add).then_inc(r.acc, 1)

                    def top(i, u, t, v, w):
                        q = filled(i)
                        dve.wait_ge(r.prod, i + 1)
                        after(dve, r.log, i, R)
                        after(dve, r.out, i, R)
                        dve.tensor_tensor(t_sb[0:q, v, :, :], ps_z[v][0:q, 0:2 * COUT].rearrange("p (j f) -> p j f", j=2),
                                          bias2[0:q, :, :], ALU.add).then_inc(s_logit, 1)
                        dve.wait_ge(s_logit, i + 1)
                        dve.tensor_reduce(neg_max[0:q, v, :], t_sb[0:q, v, :, :], AX_X, ALU.max, negate=True).then_inc(r.top, 1)

                    def final(i, u, t, v, w):
                        q = filled(i)
                        dve.wait_ge(r.log, i + 1)
                        free(dve, r.stored[v], w * 16)
                        dve.tensor_tensor(soft_shift[0:q, v, :], neg_max[0:q, v, :], log_sum[0:q, v, :], ALU.subtract).then_inc(s_shift2, 1)
                        dve.wait_ge(s_shift2, i + 1)
                        for j in range(2):
                            ins = dve.scalar_tensor_tensor(out=out_sb[0:q, v, j, :], in0=t_sb[0:q, v, j, :],
                                                           scalar=soft_shift[0:q, v, j:j + 1], in1=x_in[0:q, u, j, :],
                                                           op0=ALU.add, op1=ALU.add)
                        ins.then_inc(r.out, 1)

                    st = [(4, item(stat)), (2, item(rstd))] if l == 0 else []
                    if kind == "e":
                        return st + [(0, item(messages))]
                    if l < 2:
                        return st + [(1, item(select)), (0, item(sums))]
                    return [(1, item(top)), (2, item(select)), (0, item(final))]

                pipeline(dve, PAIRS, stages(edge[l], "e"))
                pipeline(dve, BLOCKS, stages(node[l], "n"))
                if l < 2:
                    base = 12 * l
                    n_bn = [base]

                    def step(ins):
                        ins.then_inc(s_bn, 1)
                        n_bn[0] += 1
                        dve.wait_ge(s_bn, n_bn[0])

                    gam, bet, bias = (cols_in[:, 3 * l + c, :] for c in range(3))
                    T = lambda c: bn_tmp[:, c, :]
                    dve.wait_ge(s_bn_pe, l + 1)
                    step(dve.tensor_scalar(T(0), ps_m[0][:, 0:2], 1.0 / N, None, ALU.mult))
                    step(dve.tensor_scalar(T(1), ps_m[0][:, 2:4], 1.0 / N, None, ALU.mult))
                    step(dve.tensor_tensor(T(2), T(0), T(0), ALU.mult))
                    step(dve.tensor_tensor(T(3), T(1), T(2), ALU.subtract))
                    step(dve.tensor_scalar(T(4), T(3), 0.0, None, ALU.max))
                    step(dve.tensor_tensor(T(6), T(0), bias, ALU.add))
                    dve.wait_ge(s_bn_sqrt, l + 1)
                    step(dve.reciprocal(T(7), T(5)))
                    step(dve.tensor_tensor(scale_c[:, l, :], T(7), gam, ALU.mult))
                    step(dve.tensor_tensor(T(8), bias, T(6), ALU.subtract))
                    step(dve.tensor_tensor(T(9), T(8), scale_c[:, l, :], ALU.mult))
                    step(dve.memset(acc_z[:, :], 0.0))
                    step(dve.memset(acc_sq[:, :], 0.0))
                    dve.tensor_tensor(shift_c[:, l, :], T(9), bet, ALU.add).then_inc(s_bn_ready, 1)



_INS = ['x', 'src', 'dst', 'L0_gnn_Wl0', 'L0_gnn_bl0', 'L0_gnn_Wr0', 'L0_gnn_gamma0', 'L0_gnn_beta0', 'L0_gnn_Wl1',
        'L0_gnn_bl1', 'L0_gnn_Wr1', 'L0_gnn_gamma1', 'L0_gnn_beta1', 'L0_gnn_Wl2', 'L0_gnn_bl2', 'L0_gnn_Wr2']


def kernel(**inputs):
    import numpy as _np
    import concourse.bacc as _bacc
    from concourse import mybir as _mybir
    from concourse.bass_utils import run_bass_kernel_spmd as _run

    nc = _bacc.Bacc("TRN2", target_bir_lowering=False, num_devices=1)
    arrays, args = {}, []
    for name in _INS:
        a = _np.ascontiguousarray(inputs[name])
        arrays[f"in_{name}"] = a
        args.append(nc.dram_tensor(f"in_{name}", a.shape, _mybir.dt.from_np(a.dtype), kind="ExternalInput").ap())
    args.append(nc.dram_tensor("out_dram", inputs["x"].shape, _mybir.dt.float32, kind="ExternalOutput").ap())
    gnn_kernel(nc, *args)
    r = _run(nc, [arrays], core_ids=[0])
    return r.results[0]["out_dram"]
```

```python
from contextlib import ExitStack

import concourse.bass as bass
from concourse import mybir

F32 = mybir.dt.float32
I32 = mybir.dt.int32
F32R = mybir.dt.float32r
ALU = mybir.AluOpType
ACT = mybir.ActivationFunctionType
AX_X = mybir.AxisListType.X

P = 128
EPS = 1e-5
PAD_DST = float(1 << 20)


def gnn_kernel(nc, x, src, dst, Wl0, bl0, Wr0, gamma0, beta0, Wl1, bl1, Wr1, gamma1, beta1, Wl2, bl2, Wr2, out):
    N, CIN = x.shape
    E = src.shape[0]
    HID = Wl0.shape[0]
    COUT = Wl2.shape[0]
    NODES = 2 * P
    BLOCKS = -(-N // NODES)
    TAIL_P = (N - (BLOCKS - 1) * NODES) // 2
    ROW = 2 * P
    PAIRS = -(-E // ROW)
    EPAD = PAIRS * ROW
    TILES = 2 * PAIRS
    GROUPS = -(-(BLOCKS + 1) // PAIRS)
    U = 6
    R = 3
    LAST_ROW = E - (PAIRS - 1) * ROW
    LINE_ROWS = max(n for n in range(1, 9) if PAIRS % n == 0)
    LINE = LINE_ROWS * ROW
    LINES = PAIRS // LINE_ROWS
    assert CIN == P and COUT == P and HID == 2 * P and N % 2 == 0 and PAIRS <= P
    assert GROUPS * PAIRS > BLOCKS

    K_IN = [CIN, HID, HID]
    K_OUT = [HID, HID, COUT]
    CH = [k // P for k in K_IN]

    z_dram = [nc.dram_tensor(f"z{n}", [N, HID], F32, kind="Internal").ap() for n in range(2)]
    y_dram = [nc.dram_tensor(f"y{n}", [EPAD + P, K_OUT[n] + 1], F32, kind="Internal").ap() for n in range(3)]
    dst_rows_dram = nc.dram_tensor("dst_rows", [PAIRS + 1, ROW], F32, kind="Internal").ap()
    unsorted_dram = nc.dram_tensor("unsorted", [EPAD], F32, kind="Internal").ap()
    sorted_dram = nc.dram_tensor("sorted", [EPAD, 2], F32, kind="Internal").ap()
    start_dram = nc.dram_tensor("starts", [PAIRS, GROUPS], I32, kind="Internal").ap()

    with ExitStack() as ctx:
        def sb(name, shape, dt=F32):
            return ctx.enter_context(nc.sbuf_tensor(name, shape, dt))

        def sem(name):
            return ctx.enter_context(nc.semaphore(name))

        def sems(name, n):
            return [sem(f"{name}{i}") for i in range(n)]

        ps_t = [ctx.enter_context(nc.psum_tensor(f"ps_t{i}", [P, 512], F32)) for i in range(R)]
        ps_z = [ctx.enter_context(nc.psum_tensor(f"ps_z{i}", [P, 512], F32)) for i in range(R)]
        ps_m = [ctx.enter_context(nc.psum_tensor(f"ps_m{i}", [P, 512], F32)) for i in range(2)]

        ident = sb("ident", [P, P])
        ones = sb("ones", [P, P])
        node_of_col = sb("node_of_col", [P, 2, P])
        eps_col = sb("eps_col", [P, 1])
        block_base = sb("block_base", [P, BLOCKS])
        w_raw = sb("w_raw", [P, 6, 2, HID])
        wT = sb("wT", [P, 6, 2, HID])
        cols_in = sb("cols_in", [P, 6, 2])
        bias2 = sb("bias2", [P, 2, COUT])
        scale_c = sb("scale_c", [P, 2, 2])
        shift_c = sb("shift_c", [P, 2, 2])
        bn_tmp = sb("bn_tmp", [P, 10, 2])

        src_i = sb("src_i", [P, ROW], I32)
        dst_i = sb("dst_i", [P, ROW], I32)
        src_f = sb("src_f", [P, ROW])
        dst_f = sb("dst_f", [P, ROW])
        dst_prev = sb("dst_prev", [P, ROW])
        dst_next = sb("dst_next", [P, ROW])
        edge_no = sb("edge_no", [P, ROW])
        next_i = sb("next_i", [P, ROW], I32)
        next_f = sb("next_f", [P, ROW])
        descents = sb("descents", [P, 1])
        unsorted = sb("unsorted_flag", [1, 1], I32)
        line = sb("line", [P, LINE])
        line_no = sb("line_no", [P, LINE])
        earlier = sb("earlier", [P, LINE])
        same = sb("same", [P, LINE])
        line_base = sb("line_base", [P, 1])
        edge_col = sb("edge_col", [P, TILES])
        pair_col = sb("pair_col", [P, TILES, 2])
        rank = sb("rank", [P, TILES])
        rank_part = sb("rank_part", [P, 2])
        rank_i = sb("rank_i", [P, TILES], I32)
        rank_now = sb("rank_now", [P, 1], I32)
        pair_now = sb("pair_now", [P, 2])
        sorted_rows = sb("sorted_rows", [P, ROW, 2])
        run_a = sb("run_a", [P, ROW])
        run_b = sb("run_b", [P, ROW])
        run_first = sb("run_first", [P, ROW])
        run_last = sb("run_last", [P, ROW])
        inv_cnt = sb("inv_cnt", [P, ROW])
        row_ends = sb("row_ends", [P, 2])
        row_line = sb("row_line", [1, 4, P])
        carry = sb("carry", [P, 2])
        diag = sb("diag", [P, P])
        thresholds = sb("thresholds", [P, GROUPS])
        coarse = sb("coarse", [P, GROUPS])
        coarse_i = sb("coarse_i", [P, GROUPS], I32)
        found_row = sb("found_row", [P, GROUPS, ROW])
        fine = sb("fine", [P, GROUPS])
        scratch = sb("scratch", [P, ROW])
        start_i = sb("start_i", [P, GROUPS], I32)
        start_line = sb("start_line", [1, PAIRS * GROUPS], I32)
        start_f = sb("start_f", [1, PAIRS * GROUPS])
        more_f = sb("more_f", [1, BLOCKS])
        more_i = sb("more_i", [1, BLOCKS], I32)
        more_r = sb("more_r", [1, BLOCKS])
        before_f = sb("before_f", [1, BLOCKS])
        before_i = sb("before_i", [1, BLOCKS], I32)
        line_of_ones = sb("line_of_ones", [1, BLOCKS])
        any_f = sb("any_f", [1, 1])
        any_more = sb("any_more", [1, 1], I32)
        win_more = sb("win_more", [P, HID + 1])
        sel_more = sb("sel_more", [P, 2, P])
        src_col = sb("src_col", [P, TILES], I32)
        dst_col = sb("dst_col", [P, TILES])
        inv_col = sb("inv_col", [P, TILES])
        idx_ring = sb("idx_ring", [P, U, 2], I32)
        y_pad = sb("y_pad", [P, HID + 1])

        rows_in = sb("rows_in", [P, U, 2 * HID])
        x_in = sb("x_in", [P, U, 2 * CIN])
        win = sb("win", [P, U, HID + 1])
        ln_stats = sb("ln_stats", [P, U, 2, 6])
        ln_mv = sb("ln_mv", [P, U, 2, 2])
        ln_std = sb("ln_std", [P, U, 2])
        ln_rstd = sb("ln_rstd", [P, U, 2])
        ln_shift = sb("ln_shift", [P, U, 2])
        h_rows = sb("h_rows", [P, R, 2, CIN])
        hT = sb("hT", [P, R, 2, 2, P])
        sel = sb("sel", [P, R, 2, P])
        sel_r = sb("sel_r", [P, R, 2, P], F32R)
        win_hi = sb("win_hi", [P, R, HID], F32R)
        win_lo = sb("win_lo", [P, R, HID], F32R)
        z_sb = sb("z_sb", [P, U, 2 * HID])
        z_sq = sb("z_sq", [P, R, 512])
        y_sb = sb("y_sb", [P, R, 2, HID + 1])
        acc_z = sb("acc_z", [P, 512])
        acc_sq = sb("acc_sq", [P, 512])
        t_sb = sb("t_sb", [P, R, 2, COUT])
        e_sb = sb("e_sb", [P, R, 2, COUT])
        neg_max = sb("neg_max", [P, R, 2])
        exp_sum = sb("exp_sum", [P, R, 2])
        log_sum = sb("log_sum", [P, R, 2])
        soft_shift = sb("soft_shift", [P, R, 2])
        out_sb = sb("out_sb", [P, U, 2 * COUT])

        s_const = sem("s_const")
        s_params = sem("s_params")
        s_pool = sem("s_pool")
        s_wt = sem("s_wt")
        s_wc = sem("s_wc")
        s_edges = sem("s_edges")
        s_dstf = sem("s_dstf")
        s_shift = sem("s_shift")
        s_flag_dve = sem("s_flag_dve")
        s_hi = sem("s_hi")
        s_meta = sem("s_meta")
        s_meta_pe = sem("s_meta_pe")
        s_found = sem("s_found")
        s_start = sem("s_start")
        s_ypad = sem("s_ypad")
        s_bn_pe = sem("s_bn_pe")
        s_bn = sem("s_bn")
        s_bn_sqrt = sem("s_bn_sqrt")
        s_bn_ready = sem("s_bn_ready")

        def uses(count, slot, slots):
            return (count - slot + slots - 1) // slots

        class Ring:
            def __init__(self, layer, count, per_use):
                self.layer, self.count, self.per_use = layer, count, per_use

            def landed(self, slot, turn):
                return (turn + 1 + self.layer * uses(self.count, slot, U)) * self.per_use

            def window(self, slot, turn):
                return (turn + 1 + self.layer * uses(self.count, slot, U)) * 16

            def kept(self, slot, turn):
                return (turn + self.layer * uses(self.count, slot, R)) * 16

            def all_kept(self, slot):
                return self.kept(slot, uses(self.count, slot, R))

            def twos(self, two):
                count = (self.count + 1) // 2
                return uses(count, two, U // 2) + (self.count % 2 == 0 and two == (count - 1) % (U // 2))

            def two_moved(self, slot, turn, layer=None):
                return (turn + (self.layer if layer is None else layer) * self.twos(slot // 2)) * 16

            def here(self, i, slot, turn, layer=None):
                in_two_transfers = isinstance(i, int) and self.count % 2 == 0 and i >= self.count - 2
                return self.two_moved(slot, turn + 1 + in_two_transfers, layer)

            def all_moved(self, two):
                return (self.layer + 1) * self.twos(two) * 16

        dma_sems = {"e": (sems("e_loaded", U), sems("e_stored", R)),
                    "n": (sems("n_loaded", U // 2), sems("n_stored", U // 2))}
        window_sems = sems("n_window", U)
        edge, node = [], []
        for l in range(3):
            for kind, into in (("e", edge), ("n", node)):
                r = Ring(l, *((PAIRS, 32) if kind == "e" else (BLOCKS, 16)))
                r.loaded, r.stored = dma_sems[kind]
                r.turned = sem(f"{kind}{l}_turned")
                r.hT = sem(f"{kind}{l}_hT")
                r.prod = sem(f"{kind}{l}_prod")
                r.out = sem(f"{kind}{l}_out")
                if l == 0:
                    r.stat = sem(f"{kind}{l}_stat")
                    r.std = sem(f"{kind}{l}_std")
                    r.rstd = sem(f"{kind}{l}_rstd")
                    r.rows = sem(f"{kind}{l}_rows")
                if kind == "e":
                    r.idx = sem(f"e{l}_idx")
                else:
                    r.win = window_sems
                    r.sel = sem(f"n{l}_sel")
                    r.more_loaded = sem(f"n{l}_more_loaded")
                    r.more_sel = sem(f"n{l}_more_sel")
                    r.more_done = sem(f"n{l}_more_done")
                    if l < 2:
                        r.acc = sem(f"n{l}_acc")
                        r.acc_z = sem(f"n{l}_acc_z")
                    else:
                        r.top = sem("n2_top")
                        r.x = sems("n2_x", U // 2)
                        r.log = sem("n2_log")
                into.append(r)
        s_chain = sem("s_chain")

        s_ln = {k: sem(f"s_ln_{k}") for k in "en"}
        s_rec = {k: sem(f"s_rec_{k}") for k in "en"}
        s_flag_pe = sem("s_flag_pe")
        s_flag = sem("s_flag")
        s_more = sem("s_more")
        q_out = sem("q_out")
        q_cols = sem("q_cols")
        q_line = sem("q_line")
        q_chain = sem("q_chain")
        q_used = sem("q_used")
        q_rank = sem("q_rank")
        q_now = sem("q_now")
        q_put = sem("q_put")
        q_back = sem("q_back")
        s_gate = sem("s_gate")
        s_gate_pool = sem("s_gate_pool")
        s_exp = sem("s_exp")
        s_logit = sem("s_logit")
        s_shift2 = sem("s_shift2")
        for l in range(2):
            node[l].sq = sem(f"n{l}_sq")

        S_CONST = 16
        META_SORTED = 3
        META_ENDS = 10
        META_DIAG = 11
        META_LINE = 15
        META_COARSE = 18
        META_INV = 25
        META_COLS = 26
        META_START = 27
        MORE_READY = 8
        SPLIT = [False, True, False]

        def is_unsorted(eng):
            eng.wait_ge(s_flag, 1)
            return eng.value_load(unsorted[0:1, 0:1], min_val=0, max_val=EPAD)

        def has_more(eng):
            eng.wait_ge(s_more, MORE_READY)
            return eng.value_load(any_more[0:1, 0:1], min_val=0, max_val=TILES)

        def more_of(eng, i):
            n = eng.value_load(more_i[0:1, bass.ds(i, 1)], min_val=0, max_val=TILES)
            before = eng.value_load(before_i[0:1, bass.ds(i, 1)], min_val=0, max_val=TILES)
            return n, before

        def for_each_more(eng, i, body):
            n, before = more_of(eng, i)
            with eng.If(n > 0):
                with eng.Fori(0, n) as w:
                    body(w, before + w)

        def if_more(eng, flag, count, stages):
            with eng.If(flag > 0):
                pipeline(eng, count, stages(True))
            with eng.Else():
                pipeline(eng, count, stages(False))

        def pipeline(eng, count, stages):
            most = max(o for o, _ in stages)
            full = (count - 1 - most) // U

            def step(i):
                for o, stage in stages:
                    if 0 <= i + o < count:
                        stage(i + o)

            for i in range(-most, U):
                step(i)
            with eng.Fori(1, full) as k:
                for r in range(U):
                    for o, stage in stages:
                        stage((r + o) + k * U, slot=(r + o) % U, turn=k + (r + o) // U)
            for i in range(full * U, count):
                step(i)

        def item(fn):
            def stage(i, slot=None, turn=None):
                if slot is None:
                    slot, turn = i % U, i // U
                fn(i, slot, turn, slot % R, turn * (U // R) + slot // R)
            return stage

        def two(fn):
            def stage(i, slot=None, turn=None):
                if slot is None:
                    slot, turn = i % U, i // U
                if slot % 2 == 0:
                    fn(i, slot, turn)
            return stage

        def free(eng, s, value):
            if isinstance(value, int) and value <= 0:
                return
            eng.wait_ge(s, value)

        def after(eng, s, i, lag):
            if isinstance(i, int):
                if i >= lag:
                    eng.wait_ge(s, i - lag + 1)
                return
            eng.wait_ge(s, i + (1 - lag))

        def rows_here(r, kind, i, u, t):
            return (r.loaded[u], r.landed(u, t)) if kind == "e" else (r.loaded[u // 2], r.here(i, u, t))

        block = ctx.enter_context(nc.Block())

        def filled(i):
            return TAIL_P if isinstance(i, int) and i == BLOCKS - 1 else P

        W_ALL = [Wl0, Wr0, Wl1, Wr1, Wl2, Wr2]

        def y_rows(l, i):
            return y_dram[l][bass.ds(i * ROW, ROW), :].rearrange("(a p) f -> p a f", a=2)

        def two_blocks(eng, dram, sbuf, width, i, u, s, store=False):
            if isinstance(i, int) and i + 1 >= BLOCKS - 1:
                for b in range(i, BLOCKS):
                    q = filled(b)
                    there = dram[b * NODES:b * NODES + 2 * q, :].rearrange("(p j) f -> p (j f)", j=2)
                    here = sbuf[0:q, u + b - i, 0:2 * width]
                    eng.dma_start(*((there, here) if store else (here, there))).then_inc(s, 16)
                return
            there = dram[bass.ds(i * NODES, 2 * NODES), :].rearrange("(b p j) f -> p b (j f)", b=2, j=2)
            here = sbuf[:, u:u + 2, 0:2 * width]
            eng.dma_start(*((there, here) if store else (here, there))).then_inc(s, 16)

        @block.sync
        def _(sp):
            sp.wait_ge(s_const, 3)
            for a, t in ((src, src_i), (dst, dst_i)):
                sp.dma_start(t[0:PAIRS - 1, :], a[0:(PAIRS - 1) * ROW].rearrange("(r c) -> r c", c=ROW)).then_inc(s_edges, 16)
                sp.dma_start(t[PAIRS - 1:PAIRS, 0:LAST_ROW], a[(PAIRS - 1) * ROW:E].rearrange("(r c) -> r c", r=1)).then_inc(s_edges, 16)
            sp.dma_start(next_i[0:PAIRS - 1, :], dst[1:(PAIRS - 1) * ROW + 1].rearrange("(r c) -> r c", c=ROW)).then_inc(s_edges, 16)
            sp.dma_start(next_i[PAIRS - 1:PAIRS, 0:LAST_ROW - 1], dst[(PAIRS - 1) * ROW + 1:E].rearrange("(r c) -> r c", r=1)).then_inc(s_edges, 16)
            for m, w in enumerate(W_ALL):
                o, k = w.shape
                sp.dma_start(w_raw[:, m, 0:o // P, 0:k], w.rearrange("(c p) k -> p c k", p=P)).then_inc(s_params, 16)
            with nc.allow_non_contiguous_dma(reason="a few hundred values"):
                for m, v in enumerate((gamma0, beta0, bl0, gamma1, beta1, bl1)):
                    sp.dma_start(cols_in[:, m, :], v.rearrange("(c p) -> p c", p=P)).then_inc(s_params, 16)
            for j in range(2):
                sp.dma_start(bias2[:, j, :], bl2.rearrange("(a f) -> a f", a=1).to_broadcast([P, COUT])).then_inc(s_params, 16)
            flag = is_unsorted(sp)
            with sp.If(flag > 0):
                sp.dma_start(unsorted_dram.rearrange("(r c) -> r c", c=ROW), dst_f[0:PAIRS, :]).then_inc(q_out, 16)
                sp.wait_ge(q_out, 16)
                with sp.Fori(0, LINES) as c:
                    sp.wait_ge(q_used, c + 1)
                    sp.dma_start(line[:, :], unsorted_dram[bass.ds(c * LINE, LINE)].rearrange("(a n) -> a n", a=1)
                                 .to_broadcast([P, LINE])).then_inc(q_line, 16)
                sp.wait_ge(q_put, 16 * TILES)
                sp.dma_start(sorted_rows[0:PAIRS, :, :], sorted_dram.rearrange("(r c) v -> r c v", c=ROW)).then_inc(q_back, 16)
            sp.wait_ge(s_meta, META_SORTED)
            sp.dma_start(dst_rows_dram[0:PAIRS, :], dst_f[0:PAIRS, :]).then_inc(s_dstf, 16)
            sp.wait_ge(s_const, 6)
            sp.dma_start(dst_rows_dram[PAIRS:PAIRS + 1, :], scratch[0:1, :]).then_inc(s_dstf, 16)
            sp.wait_ge(s_dstf, 32)
            flat = dst_rows_dram.rearrange("r c -> (r c)")
            sp.dma_start(dst_prev[1:PAIRS, :], flat[ROW - 1:EPAD - 1].rearrange("(r c) -> r c", c=ROW)).then_inc(s_shift, 16)
            sp.dma_start(dst_prev[0:1, 1:ROW], flat[0:ROW - 1].rearrange("(r c) -> r c", r=1)).then_inc(s_shift, 16)
            sp.dma_start(dst_next[0:PAIRS, :], flat[1:EPAD + 1].rearrange("(r c) -> r c", c=ROW)).then_inc(s_shift, 16)
            for l in range(3):
                sp.dma_start(y_dram[l][EPAD:EPAD + P, :], y_pad[:, HID - K_OUT[l]:HID + 1]).then_inc(s_ypad, 16)
            sp.wait_ge(s_meta, META_START)
            sp.dma_start(start_dram, start_i[0:PAIRS, :]).then_inc(s_start, 16)
            sp.wait_ge(s_start, 16)
            sp.dma_start(start_line[0:1, :], start_dram.rearrange("r g -> (r g)").rearrange("(a n) -> a n", a=1)).then_inc(s_start, 16)
            sp.wait_ge(s_start, 32)
            sp.wait_ge(s_ypad, 48)

            for l in range(3):
                e, n = edge[l], node[l]
                W = K_OUT[l]

                def store_messages(i, u, t, v, w):
                    sp.wait_ge(e.out, i + 1)
                    sp.dma_start(y_rows(l, i), y_sb[:, v, :, 0:W + 1]).then_inc(e.stored[v], 16)

                pipeline(sp, PAIRS, [(0, item(store_messages))])
                for v in range(R):
                    sp.wait_ge(e.stored[v], e.all_kept(v))

                def load_rows(i, u, t):
                    after(sp, n.rows if l == 0 else n.turned, min(i + 1, BLOCKS - 1) if isinstance(i, int) else i + 1, U)
                    two_blocks(sp, x if l == 0 else z_dram[l - 1], rows_in, K_IN[l], i, u, n.loaded[u // 2])

                def load_window(i, u, t, v, w):
                    after(sp, n.prod, i, U)
                    start = sp.value_load(start_line[0:1, bass.ds(i, 1)], min_val=0, max_val=EPAD)
                    sp.dma_start(win[:, u, 0:W + 1], y_dram[l][bass.ds(start, P), :]).then_inc(n.win[u], 16)

                def store_blocks(i, u, t):
                    sp.wait_ge(n.out, min(i + 2, BLOCKS) if isinstance(i, int) else i + 2)
                    two_blocks(sp, z_dram[l] if l < 2 else out, z_sb if l < 2 else out_sb, HID if l < 2 else COUT, i, u,
                               n.stored[u // 2], store=True)

                pipeline(sp, BLOCKS, [(8, two(load_rows)), (7, item(load_window)), (0, two(store_blocks))])
                for c in range(U // 2):
                    sp.wait_ge(n.stored[c], n.all_moved(c))


        @block.gpsimd
        def _(pool):
            pool.memset(src_i[:, :], 0).then_inc(s_const, 1)
            pool.memset(dst_i[:, :], int(PAD_DST)).then_inc(s_const, 1)
            pool.memset(next_i[:, :], int(PAD_DST)).then_inc(s_const, 1)
            pool.memset(scratch[:, :], PAD_DST).then_inc(s_const, 1)
            pool.memset(y_pad[:, :], -1.0).then_inc(s_const, 1)
            pool.memset(dst_prev[:, :], -1.0).then_inc(s_const, 1)
            pool.memset(ident[:, :], 0.0).then_inc(s_pool, 1)
            pool.memset(ones[:, :], 1.0).then_inc(s_const, 1)
            pool.memset(line_of_ones[:, :], 1.0).then_inc(s_const, 1)
            pool.iota(line_no[:, :], pattern=[[1, LINE]], base=0, channel_multiplier=0,
                      allow_small_or_imprecise_dtypes=True).then_inc(s_const, 1)
            pool.iota(edge_col[:, :], pattern=[[P, TILES]], base=0, channel_multiplier=1,
                      allow_small_or_imprecise_dtypes=True).then_inc(s_const, 1)
            pool.wait_ge(s_pool, 1)
            pool.affine_select(out=ident[:, :], in_=ident[:, :], compare_op=ALU.not_equal, fill=1.0,
                               base=0, pattern=[[-1, P]], channel_multiplier=1).then_inc(s_const, 1)
            pool.iota(edge_no[:, :], pattern=[[1, ROW]], base=0, channel_multiplier=ROW,
                      allow_small_or_imprecise_dtypes=True).then_inc(s_const, 1)
            pool.iota(thresholds[:, :], pattern=[[NODES, GROUPS]], base=0, channel_multiplier=GROUPS * NODES,
                      allow_small_or_imprecise_dtypes=True).then_inc(s_const, 1)
            pool.iota(node_of_col[:, :, :], pattern=[[1, 2], [2, P]], base=0, channel_multiplier=0,
                      allow_small_or_imprecise_dtypes=True).then_inc(s_const, 1)
            pool.iota(block_base[:, :], pattern=[[NODES, BLOCKS]], base=0, channel_multiplier=0,
                      allow_small_or_imprecise_dtypes=True).then_inc(s_const, 1)
            pool.memset(eps_col[:, :], EPS).then_inc(s_const, 1)
            flag = is_unsorted(pool)
            with pool.If(flag > 0):
                pool.wait_ge(q_rank, 1)
                with pool.Fori(0, TILES) as t:
                    pool.tensor_copy(rank_now[:, :], rank_i[:, bass.ds(t, 1)]).then_inc(q_now, 1)
                    pool.tensor_copy(pair_now[:, :], pair_col[:, bass.ds(t, 1), :].rearrange("p a v -> p (a v)")).then_inc(q_now, 1)
                    pool.wait_ge(q_now, t * 2 + 2)
                    pool.sem_inc(s_gate_pool, 1)
                    pool.indirect_dma_start(out=sorted_dram, out_offset=bass.IndirectOffsetOnAxis(ap=rank_now[:, 0:1], axis=0),
                                            in_=pair_now[:, :], in_offset=None, bounds_check=EPAD - 1, oob_is_err=False).then_inc(q_put, 16)
                    pool.wait_ge(q_put, t * 16 + 16)
                    pool.sem_inc(s_gate_pool, 1)
            pool.wait_ge(s_meta, META_COARSE)
            pool.wait_ge(s_dstf, 32)
            for g in range(GROUPS):
                pool.indirect_dma_start(out=found_row[0:PAIRS, g, :], out_offset=None, in_=dst_rows_dram,
                                        in_offset=bass.IndirectOffsetOnAxis(ap=coarse_i[0:PAIRS, g:g + 1], axis=0),
                                        bounds_check=PAIRS, oob_is_err=False).then_inc(s_found, 16)
            pool.wait_ge(s_meta, META_COLS)
            for l in range(3):
                e = edge[l]
                if l > 0:
                    for c in range(U // 2):
                        pool.wait_ge(node[l - 1].stored[c], node[l - 1].all_moved(c))
                source = x if l == 0 else z_dram[l - 1]

                def gather(i, u, t, v, w):
                    after(pool, e.rows if l == 0 else e.turned, i, U)
                    pool.sem_inc(s_gate_pool, 1)
                    pool.tensor_copy(idx_ring[:, u, :], src_col[:, bass.ds(i * 2, 2)]).then_inc(e.idx, 1)
                    pool.wait_ge(e.idx, i + 1)
                    pool.sem_inc(s_gate_pool, 1)
                    for a in range(2):
                        pool.indirect_dma_start(out=rows_in[:, u, a * K_IN[l]:(a + 1) * K_IN[l]], out_offset=None, in_=source,
                                                in_offset=bass.IndirectOffsetOnAxis(ap=idx_ring[:, u, a:a + 1], axis=0),
                                                bounds_check=N - 1, oob_is_err=False).then_inc(e.loaded[u], 16)

                pipeline(pool, PAIRS, [(0, item(gather))])
                n = node[l]
                W = K_OUT[l]
                if l == 0:
                    more = has_more(pool)

                def pool_stages(with_more):
                    def load_more(i, u, t, v, w):
                        def window(m, k):
                            pool.wait_ge(n.more_done, k + 1)
                            pool.sem_inc(s_gate_pool, 1)
                            start = pool.value_load(start_line[0:1, bass.ds(i, 1)], min_val=0, max_val=EPAD)
                            first = nc.s_assert_within(start + (m + 1) * P, 0, EPAD, skip_runtime_bounds_check_because=
                                                       "the block's edges reach past it")
                            pool.dma_start(win_more[:, 0:W + 1], y_dram[l][bass.ds(first, P), :]).then_inc(n.more_loaded, 16)
                        for_each_more(pool, i, window)

                    def sum_z(i, u, t, v, w):
                        q = filled(i)
                        pool.wait_ge(n.out, i + 1)
                        after(pool, n.acc_z, i, 1)
                        pool.tensor_tensor(acc_z[0:q, :], acc_z[0:q, :], z_sb[0:q, u, :], ALU.add).then_inc(n.acc_z, 1)

                    def load_x(i, u, t):
                        after(pool, n.out, min(i + 1, BLOCKS - 1) if isinstance(i, int) else i + 1, U)
                        pool.sem_inc(s_gate_pool, 1)
                        two_blocks(pool, x, x_in, CIN, i, u, n.x[u // 2])

                    return [(4, item(load_more))] * with_more + [(0, item(sum_z)) if l < 2 else (5, two(load_x))]

                if_more(pool, more, BLOCKS, pool_stages)


        @block.tensor
        def _(pe):
            pe.wait_ge(s_const, S_CONST)
            for l in range(3):
                pe.sem_inc(node[l].more_done, 1)
            pe.wait_ge(s_meta, 2)
            pe.matmul(ps_m[0][0:1, 0:1], ones[0:PAIRS, 0:1], descents[0:PAIRS, :], start=True, stop=True).then_inc(s_flag_pe, 1)
            flag = is_unsorted(pe)
            with pe.If(flag > 0):
                for c, t in enumerate((dst_f, src_f)):
                    for a in range(2):
                        mm = pe.transpose(ps_t[c][:, a * P:a * P + PAIRS], t[0:PAIRS, a * P:(a + 1) * P], ident[0:PAIRS, 0:PAIRS])
                mm.then_inc(q_cols, 1)
            pe.wait_ge(s_meta, META_ENDS)
            for c in range(2):
                mm = pe.transpose(ps_m[0][0:1, c * P:c * P + PAIRS], row_ends[0:PAIRS, c:c + 1], ident[0:PAIRS, 0:PAIRS])
            mm.then_inc(s_meta_pe, 1)
            pe.wait_ge(s_meta, META_DIAG)
            pe.matmul(ps_m[1][0:PAIRS, 0:PAIRS], ones[0:PAIRS, 0:PAIRS], diag[0:PAIRS, 0:PAIRS],
                      start=True, stop=True).then_inc(s_meta_pe, 1)
            pe.wait_ge(s_meta, META_LINE)
            for c in range(2):
                mm = pe.transpose(ps_m[0][0:PAIRS, 256 + c:257 + c], row_line[0:1, 2 + c, 0:PAIRS], ident[0:1, 0:1])
            mm.then_inc(s_meta_pe, 1)
            pe.wait_ge(s_meta, META_INV)
            for c, t in enumerate((src_f, dst_f, inv_cnt)):
                for a in range(2):
                    mm = pe.transpose(ps_t[c][:, a * P:a * P + PAIRS], t[0:PAIRS, a * P:(a + 1) * P], ident[0:PAIRS, 0:PAIRS])
            mm.then_inc(s_meta_pe, 1)
            pe.wait_ge(s_params, 16 * 14)
            g = 0
            for m, w in enumerate(W_ALL):
                o, k = w.shape
                for c in range(k // P):
                    if g >= R:
                        pe.wait_ge(s_wc, g - R + 1)
                    for h in range(o // P):
                        mm = pe.transpose(ps_z[g % R][:, h * P:(h + 1) * P], w_raw[:, m, h, c * P:(c + 1) * P], ident[:, :])
                    mm.then_inc(s_wt, 1)
                    g += 1
            pe.wait_ge(s_wc, g)
            pe.wait_ge(s_meta, META_COLS)
            more = None

            for l in range(3):
                W = K_OUT[l]

                def stages(r, kind, with_more=False):
                    def turn(i, u, t, v, w):
                        q = filled(i) if kind == "n" else P
                        if l == 0:
                            pe.wait_ge(r.rows, i + 1)
                        else:
                            pe.wait_ge(*rows_here(r, kind, i, u, t))
                        after(pe, r.hT, i, R)
                        for c in range(CH[l]):
                            for j in range(2):
                                a = h_rows[0:q, v, j, :] if l == 0 else rows_in[0:q, u, (CH[l] * j + c) * P:(CH[l] * j + c + 1) * P]
                                mm = pe.transpose(ps_t[v][:, (2 * c + j) * P:(2 * c + j) * P + q], a, ident[0:q, 0:q])
                        mm.then_inc(r.turned, 1)

                    def product(i, u, t, v, w):
                        q = filled(i) if kind == "n" else P
                        if kind == "n":
                            pe.wait_ge(r.sel, i + 1)
                            pe.wait_ge(r.win[u], r.window(u, t))
                        after(pe, r.out if kind == "e" else (r.sq if l < 2 else r.top), i, R)
                        if kind == "n" and SPLIT[l]:
                            for j in range(2):
                                for part in (win_hi, win_lo):
                                    pe.matmul(ps_z[v][0:q, j * W:(j + 1) * W], sel_r[:, v, j, 0:q], part[:, v, 0:W],
                                              start=(j == 0 and part is win_hi), stop=False, skip_group_check=True)
                        elif kind == "n":
                            for j in range(2):
                                pe.matmul(ps_z[v][0:q, j * W:(j + 1) * W], sel[:, v, j, 0:q], win[:, u, 0:W],
                                          start=(j == 0), stop=False, skip_group_check=True)

                        def window(m, k):
                            pe.wait_ge(r.more_sel, k + 1)
                            for j in range(2):
                                mm = pe.matmul(ps_z[v][0:q, j * W:(j + 1) * W], sel_more[:, j, 0:q], win_more[:, 0:W],
                                               start=False, stop=False, skip_group_check=True)
                            mm.then_inc(r.more_done, 1)

                        if with_more:
                            for_each_more(pe, i, window)
                        pe.wait_ge(r.hT, i + 1)
                        for j in range(2):
                            for c in range(CH[l]):
                                mm = pe.matmul(ps_z[v][0:q, j * W:(j + 1) * W], hT[:, v, c, j, 0:q],
                                               wT[:, 2 * l + (kind == "n"), c, 0:W],
                                               start=(kind == "e" and j == 0 and c == 0), stop=(j == 1 and c == CH[l] - 1),
                                               skip_group_check=True)
                        mm.then_inc(r.prod, 1)

                    ahead = 2 if kind == "n" and l == 2 else 0
                    return [(2 + ahead, item(turn)), (1 + ahead, item(product))]

                pipeline(pe, PAIRS, stages(edge[l], "e"))
                if l == 0:
                    more = has_more(pe)
                if_more(pe, more, BLOCKS, lambda with_more: stages(node[l], "n", with_more))
                if l < 2:
                    pe.wait_ge(node[l].acc, BLOCKS)
                    pe.wait_ge(node[l].acc_z, BLOCKS)
                    for s, acc in enumerate((acc_z, acc_sq)):
                        for c in range(2):
                            for j in range(2):
                                mm = pe.matmul(ps_m[0][:, 2 * s + c:2 * s + c + 1], acc[:, j * W + c * P:j * W + (c + 1) * P],
                                               ones[:, 0:1], start=(j == 0), stop=(j == 1), skip_group_check=True)
                    mm.then_inc(s_bn_pe, 1)


        @block.scalar
        def _(act):
            g = 0
            for m, w in enumerate(W_ALL):
                o, k = w.shape
                for c in range(k // P):
                    act.wait_ge(s_wt, g + 1)
                    act.activation(wT[:, m, c, 0:o], ps_z[g % R][:, 0:o], ACT.Copy).then_inc(s_wc, 1)
                    g += 1
            act.wait_ge(s_const, S_CONST)

            for l in range(3):
                W = K_OUT[l]
                if l > 0:
                    act.wait_ge(s_bn_ready, l)
                act.preload_act_table_set("sqrt_and_others" if l < 2 else "natural_log_exp_and_others")

                def stages(r, kind):
                    def std(i, u, t, v, w):
                        q = filled(i) if kind == "n" else P
                        act.wait_ge(r.stat, i + 1)
                        after(act, r.rstd, i, U)
                        act.activation(ln_std[0:q, u, :], ln_mv[0:q, u, :, 1], ACT.Sqrt, bias=eps_col[0:q, :]).then_inc(r.std, 1)

                    def norm(i, u, t, v, w):
                        q = filled(i) if kind == "n" else P
                        act.wait_ge(r.rstd, i + 1)
                        act.wait_ge(*rows_here(r, kind, i, u, t))
                        after(act, r.turned, i, R)
                        for j in range(2):
                            ins = act.activation(h_rows[0:q, v, j, :], rows_in[0:q, u, j * CIN:(j + 1) * CIN], ACT.Relu,
                                                 bias=ln_shift[0:q, u, j:j + 1], scale=ln_rstd[0:q, u, j:j + 1])
                        ins.then_inc(r.rows, 1)

                    def copy_hT(i, u, t, v, w):
                        q = filled(i) if kind == "n" else P
                        act.wait_ge(r.turned, i + 1)
                        after(act, r.prod, i, R)
                        for c in range(CH[l]):
                            a = ps_t[v][:, 2 * c * P:2 * (c + 1) * P].rearrange("p (j n) -> p j n", j=2)[:, :, 0:q]
                            ins = act.activation(hT[:, v, c, :, 0:q], a, ACT.Relu,
                                                 bias=shift_c[:, l - 1, c:c + 1], scale=scale_c[:, l - 1, c:c + 1])
                        ins.then_inc(r.hT, 1)

                    def copy_z(i, u, t, v, w):
                        q = filled(i)
                        act.wait_ge(r.prod, i + 1)
                        free(act, r.stored[u // 2], r.two_moved(u, t))
                        after(act, r.acc_z, i, U)
                        act.activation(z_sb[0:q, u, :], ps_z[v][0:q, :], ACT.Copy).then_inc(r.out, 1)
                        after(act, r.acc, i, R)
                        act.activation(z_sq[0:q, v, :], ps_z[v][0:q, :], ACT.Square).then_inc(r.sq, 1)

                    def soft(i, u, t, v, w):
                        q = filled(i)
                        act.wait_ge(r.top, i + 1)
                        for j in range(2):
                            ins = act.activation(e_sb[0:q, v, j, :], t_sb[0:q, v, j, :], ACT.Exp,
                                                 bias=neg_max[0:q, v, j:j + 1], accum_out=exp_sum[0:q, v, j:j + 1])
                        ins.then_inc(s_exp, 1)
                        act.wait_ge(s_exp, i + 1)
                        after(act, r.out, i, R)
                        act.activation(log_sum[0:q, v, :], exp_sum[0:q, v, :], ACT.Ln).then_inc(r.log, 1)

                    first = [(5, item(std)), (3, item(norm))] if l == 0 else [(2, item(copy_hT))]
                    if kind == "e":
                        return first
                    if l < 2:
                        return first + [(0, item(copy_z))]
                    return [(4, item(copy_hT)), (1, item(soft))]

                pipeline(act, PAIRS, stages(edge[l], "e"))
                pipeline(act, BLOCKS, stages(node[l], "n"))
                if l < 2:
                    act.wait_ge(s_bn, 6 * (l + 1) + 6 * l)
                    act.activation(bn_tmp[:, 5, :], bn_tmp[:, 4, :], ACT.Sqrt, bias=eps_col[:, :]).then_inc(s_bn_sqrt, 1)


        @block.vector
        def _(dve):
            done = [0]

            def link(ins):
                ins.then_inc(s_meta, 1)
                done[0] += 1
                dve.wait_ge(s_meta, done[0])

            R_ = slice(0, PAIRS)
            dve.wait_ge(s_edges, 96)
            dve.tensor_copy(src_f[:, :], src_i[:, :])
            dve.tensor_copy(next_f[:, :], next_i[:, :])
            link(dve.tensor_copy(dst_f[:, :], dst_i[:, :]))
            dve.tensor_tensor(next_f[R_, :], next_f[R_, :], dst_f[R_, :], ALU.is_lt).then_inc(s_flag_dve, 1)
            dve.wait_ge(s_flag_dve, 1)
            link(dve.tensor_reduce(descents[R_, :], next_f[R_, :], AX_X, ALU.add))
            dve.wait_ge(s_flag_pe, 1)
            dve.tensor_copy(unsorted[0:1, 0:1], ps_m[0][0:1, 0:1]).then_inc(s_flag, 1)
            flag = is_unsorted(dve)
            with dve.If(flag > 0):
                dve.wait_ge(q_cols, 1)
                for c in range(2):
                    dve.tensor_copy(pair_col[:, :, c].rearrange("p (r a) -> p a r", a=2),
                                    ps_t[c][:, 0:2 * P].rearrange("p (a r) -> p a r", a=2)[:, :, R_])
                dve.memset(line_base[:, :], 0.0)
                dve.memset(rank[:, :], 0.0).then_inc(q_used, 1)
                dve.wait_ge(q_used, 1)
                with dve.Fori(0, LINES) as c:
                    dve.wait_ge(q_line, c * 16 + 16)
                    dve.sem_inc(s_gate, 1)
                    with dve.Fori(0, TILES) as t:
                        done_before = (c * TILES + t) * 5

                        def follow(ins, n):
                            ins.then_inc(q_chain, 1)
                            dve.wait_ge(q_chain, done_before + n)
                            dve.sem_inc(s_gate, 1)

                        follow(dve.tensor_scalar(earlier[:, :], line_no[:, :], line_base[:, 0:1], edge_col[:, bass.ds(t, 1)],
                                                 ALU.add, ALU.is_lt), 1)
                        follow(dve.scalar_tensor_tensor(out=same[:, :], in0=line[:, :],
                                                        scalar=pair_col[:, bass.ds(t, 1), 0:1].rearrange("p a v -> p (a v)"),
                                                        in1=earlier[:, :], op0=ALU.is_equal, op1=ALU.mult,
                                                        accum_out=rank_part[:, 0:1]), 2)
                        follow(dve.tensor_scalar(same[:, :], line[:, :], pair_col[:, bass.ds(t, 1), 0:1].rearrange("p a v -> p (a v)"),
                                                 None, ALU.is_lt, ALU.add, accum_out=rank_part[:, 1:2]), 3)
                        for n in range(2):
                            follow(dve.tensor_tensor(rank[:, bass.ds(t, 1)], rank[:, bass.ds(t, 1)], rank_part[:, n:n + 1], ALU.add), 4 + n)
                    dve.tensor_scalar(line_base[:, :], line_base[:, :], float(LINE), None, ALU.add).then_inc(q_used, 1)
                    dve.wait_ge(q_used, c + 2)
                dve.tensor_copy(rank_i[:, :], rank[:, :]).then_inc(q_rank, 1)
                dve.wait_ge(q_back, 16)
                dve.tensor_copy(dst_f[R_, :], sorted_rows[R_, :, 0])
                dve.tensor_copy(src_f[R_, :], sorted_rows[R_, :, 1])
            link(dve.memset(acc_sq[:, :], 0.0))
            dve.wait_ge(s_const, S_CONST)
            dve.wait_ge(s_shift, 48)
            link(dve.tensor_tensor(run_a[R_, :], dst_f[R_, :], dst_prev[R_, :], ALU.not_equal))
            link(dve.tensor_tensor(run_a[R_, :], run_a[R_, :], edge_no[R_, :], ALU.mult))
            link(dve.tensor_tensor(run_b[R_, :], dst_f[R_, :], dst_next[R_, :], ALU.is_equal))
            link(dve.scalar_tensor_tensor(out=run_b[R_, :], in0=run_b[R_, :], scalar=PAD_DST, in1=edge_no[R_, :],
                                          op0=ALU.mult, op1=ALU.add))
            link(dve.tensor_tensor_scan(run_first[R_, :], run_a[R_, :], run_a[R_, :], 0.0, ALU.max, ALU.max))
            link(dve.tensor_tensor_scan(run_last[R_, ::-1], run_b[R_, ::-1], run_b[R_, ::-1], 4 * PAD_DST, ALU.min, ALU.min))
            dve.tensor_copy(row_ends[R_, 0:1], run_first[R_, ROW - 1:ROW])
            link(dve.tensor_copy(row_ends[R_, 1:2], run_last[R_, 0:1]))
            link(dve.tensor_scalar(diag[R_, R_], ident[R_, R_], dst_f[R_, ROW - 1:ROW], None, ALU.mult))
            dve.wait_ge(s_meta_pe, 1)
            link(dve.tensor_copy(row_line[0:1, 0:2, R_], ps_m[0][0:1, 0:2 * P].rearrange("p (c n) -> p c n", c=2)[:, :, R_]))
            link(dve.memset(row_line[0:1, 2, 0:1], 0.0))
            dve.memset(row_line[0:1, 3, PAIRS - 1:PAIRS], 4 * PAD_DST)
            link(dve.tensor_tensor_scan(row_line[0:1, 2, 1:PAIRS], row_line[0:1, 0, 0:PAIRS - 1], row_line[0:1, 0, 0:PAIRS - 1],
                                        0.0, ALU.max, ALU.max))
            link(dve.tensor_tensor_scan(row_line[0:1, 3, PAIRS - 2::-1], row_line[0:1, 1, PAIRS - 1:0:-1],
                                        row_line[0:1, 1, PAIRS - 1:0:-1], 4 * PAD_DST, ALU.min, ALU.min))
            dve.wait_ge(s_meta_pe, 2)
            link(dve.tensor_copy(diag[R_, R_], ps_m[1][R_, R_]))                         
            for g in range(GROUPS):
                ins = dve.tensor_scalar(scratch[R_, R_], diag[R_, R_], thresholds[R_, g:g + 1], None, ALU.is_lt, ALU.add,
                                        accum_out=coarse[R_, g:g + 1])
                if g < GROUPS - 1:
                    ins.then_inc(s_chain, 1)
                    dve.wait_ge(s_chain, g + 1)
            link(ins)                                                                    
            link(dve.tensor_copy(coarse_i[R_, :], coarse[R_, :]))
            dve.wait_ge(s_meta_pe, 3)
            link(dve.tensor_copy(carry[R_, :], ps_m[0][R_, 256:258]))
            link(dve.tensor_scalar(run_first[R_, :], run_first[R_, :], carry[R_, 0:1], None, ALU.max))
            link(dve.tensor_scalar(run_last[R_, :], run_last[R_, :], carry[R_, 1:2], None, ALU.min))
            link(dve.tensor_tensor(run_a[R_, :], run_last[R_, :], run_first[R_, :], ALU.subtract))
            link(dve.tensor_scalar(run_b[R_, :], run_a[R_, :], 1.0, 1.0, ALU.add, ALU.max))
            link(dve.reciprocal(inv_cnt[R_, :], run_b[R_, :]))
            link(dve.memset(acc_z[:, :], 0.0))
            dve.wait_ge(s_meta_pe, 4)
            for c, t in enumerate((src_col, dst_col, inv_col)):
                ins = dve.tensor_copy(t[:, :].rearrange("p (r a) -> p a r", a=2),
                                      ps_t[c][:, 0:2 * P].rearrange("p (a r) -> p a r", a=2)[:, :, R_])
            link(ins)
            dve.wait_ge(s_found, 16 * GROUPS)
            for g in range(GROUPS):
                dve.tensor_scalar(scratch[R_, :], found_row[R_, g, :], thresholds[R_, g:g + 1], None, ALU.is_lt, ALU.add,
                                  accum_out=fine[R_, g:g + 1]).then_inc(s_chain, 1)
                dve.wait_ge(s_chain, GROUPS + g)
            dve.scalar_tensor_tensor(out=start_i[R_, :], in0=coarse[R_, :], scalar=float(ROW), in1=fine[R_, :],
                                     op0=ALU.mult, op1=ALU.add).then_inc(s_meta, 1)
            dve.wait_ge(s_start, 32)

            def more_step(ins, n):
                ins.then_inc(s_more, 1)
                dve.wait_ge(s_more, n)

            more_step(dve.tensor_copy(start_f[:, :], start_line[:, :]), 1)
            more_step(dve.tensor_tensor(more_f[:, :], start_f[:, 1:BLOCKS + 1], start_f[:, 0:BLOCKS], ALU.subtract), 2)
            more_step(dve.tensor_scalar(more_r[:, :], more_f[:, :], 1.0 / P, -1.0 / P - 63.5 / P, ALU.mult, ALU.add), 3)
            more_step(dve.tensor_scalar(more_i[:, :], more_r[:, :], 0.0, None, ALU.max), 4)
            more_step(dve.tensor_copy(more_f[:, :], more_i[:, :]), 5)
            dve.tensor_reduce(any_f[:, :], more_f[:, :], AX_X, ALU.add)
            more_step(dve.tensor_tensor_scan(more_r[:, :], line_of_ones[:, :], more_f[:, :], 0.0, ALU.mult, ALU.add), 6)
            more_step(dve.tensor_copy(any_more[:, :], any_f[:, :]), 7)
            dve.tensor_tensor(before_i[:, :], more_r[:, :], more_f[:, :], ALU.subtract).then_inc(s_more, 1)
            more = None

            for l in range(3):
                W = K_OUT[l]

                def stages(r, kind, with_more=False):
                    def stat(i, u, t, v, w):
                        q = filled(i) if kind == "n" else P
                        dve.wait_ge(*rows_here(r, kind, i, u, t))
                        for j in range(2):
                            dve.bn_stats(ln_stats[0:q, u, j, :], rows_in[0:q, u, j * CIN:(j + 1) * CIN]).then_inc(s_ln[kind], 1)
                        after(dve, r.std, i, U)
                        dve.wait_ge(s_ln[kind], i * 2 + 2)
                        dve.sem_inc(s_gate, 1)
                        for j in range(2):
                            ins = dve.bn_aggr(ln_mv[0:q, u, j, :], ln_stats[0:q, u, j, :])
                        ins.then_inc(r.stat, 1)

                    def rstd(i, u, t, v, w):
                        q = filled(i) if kind == "n" else P
                        dve.wait_ge(r.std, i + 1)
                        after(dve, r.rows, i, U)
                        dve.reciprocal(ln_rstd[0:q, u, :], ln_std[0:q, u, :]).then_inc(s_rec[kind], 1)
                        dve.wait_ge(s_rec[kind], i + 1)
                        dve.scalar_tensor_tensor(out=ln_shift[0:q, u, :], in0=ln_mv[0:q, u, :, 0], scalar=-1.0,
                                                 in1=ln_rstd[0:q, u, :], op0=ALU.mult, op1=ALU.mult).then_inc(r.rstd, 1)

                    def copy_hT(i, u, t, v, w):
                        q = filled(i) if kind == "n" else P
                        dve.wait_ge(r.turned, i + 1)
                        after(dve, r.prod, i, R)
                        dve.tensor_copy(hT[:, v, 0, :, 0:q], ps_t[v][:, 0:2 * P].rearrange("p (j n) -> p j n", j=2)[:, :, 0:q]).then_inc(r.hT, 1)

                    def messages(i, u, t, v, w):
                        dve.wait_ge(r.prod, i + 1)
                        free(dve, r.stored[v], r.kept(v, w))
                        dve.tensor_copy(y_sb[:, v, :, W:W + 1], dst_col[:, bass.ds(i * 2, 2)].rearrange("p (a o) -> p a o", o=1))
                        for a in range(2):
                            ins = dve.tensor_scalar(y_sb[:, v, a, 0:W], ps_z[v][:, a * W:(a + 1) * W],
                                                    inv_col[:, bass.ds(i * 2 + a, 1)], None, ALU.mult)
                        ins.then_inc(r.out, 1)

                    def select(i, u, t, v, w):
                        dve.wait_ge(r.win[u], r.window(u, t))
                        after(dve, r.prod, i, R)
                        if SPLIT[l]:
                            dve.tensor_copy(win_hi[:, v, :], win[:, u, 0:W]).then_inc(s_hi, 1)
                        ins = dve.tensor_scalar((sel_r if SPLIT[l] else sel)[:, v, :, :], node_of_col[:, :, :],
                                                block_base[:, bass.ds(i, 1)], win[:, u, W:W + 1], ALU.add, ALU.is_equal)
                        if SPLIT[l]:
                            dve.wait_ge(s_hi, i + 1)
                            ins = dve.tensor_tensor(win_lo[:, v, :], win[:, u, 0:W], win_hi[:, v, :].bitcast(F32), ALU.subtract)
                        ins.then_inc(r.sel, 1)

                        def window(m, k):
                            dve.wait_ge(r.more_loaded, k * 16 + 16)
                            dve.sem_inc(s_gate, 1)
                            dve.tensor_scalar(sel_more[:, :, :], node_of_col[:, :, :], block_base[:, bass.ds(i, 1)],
                                              win_more[:, W:W + 1], ALU.add, ALU.is_equal).then_inc(r.more_sel, 1)

                        if with_more:
                            for_each_more(dve, i, window)

                    def sums(i, u, t, v, w):
                        q = filled(i)
                        dve.wait_ge(r.sq, i + 1)
                        after(dve, r.acc, i, 1)
                        dve.tensor_tensor(acc_sq[0:q, :], acc_sq[0:q, :], z_sq[0:q, v, :], ALU.add).then_inc(r.acc, 1)

                    def top(i, u, t, v, w):
                        q = filled(i)
                        dve.wait_ge(r.prod, i + 1)
                        after(dve, r.log, i, R)
                        after(dve, r.out, i, R)
                        dve.tensor_tensor(t_sb[0:q, v, :, :], ps_z[v][0:q, 0:2 * COUT].rearrange("p (j f) -> p j f", j=2),
                                          bias2[0:q, :, :], ALU.add).then_inc(s_logit, 1)
                        dve.wait_ge(s_logit, i + 1)
                        dve.tensor_reduce(neg_max[0:q, v, :], t_sb[0:q, v, :, :], AX_X, ALU.max, negate=True).then_inc(r.top, 1)

                    def final(i, u, t, v, w):
                        q = filled(i)
                        dve.wait_ge(r.log, i + 1)
                        dve.wait_ge(r.x[u // 2], r.here(i, u, t, 0))
                        free(dve, r.stored[u // 2], r.two_moved(u, t))
                        dve.tensor_tensor(soft_shift[0:q, v, :], neg_max[0:q, v, :], log_sum[0:q, v, :], ALU.subtract).then_inc(s_shift2, 1)
                        dve.wait_ge(s_shift2, i + 1)
                        for j in range(2):
                            ins = dve.scalar_tensor_tensor(out=out_sb[0:q, u, j * COUT:(j + 1) * COUT], in0=t_sb[0:q, v, j, :],
                                                           scalar=soft_shift[0:q, v, j:j + 1], in1=x_in[0:q, u, j * CIN:(j + 1) * CIN],
                                                           op0=ALU.add, op1=ALU.add)
                        ins.then_inc(r.out, 1)

                    st = [(6, item(stat)), (4, item(rstd))] if l == 0 else []
                    if kind == "e":
                        return st + [(2, item(copy_hT))] * (l == 0) + [(0, item(messages))]
                    if l == 0:
                        return st + [(3, item(select)), (2, item(copy_hT)), (0, item(sums))]
                    if l == 1:
                        return [(2, item(select)), (0, item(sums))]
                    return [(4, item(select)), (2, item(top)), (0, item(final))]

                pipeline(dve, PAIRS, stages(edge[l], "e"))
                if l == 0:
                    more = has_more(dve)
                if_more(dve, more, BLOCKS, lambda with_more: stages(node[l], "n", with_more))
                if l < 2:
                    base = 12 * l
                    n_bn = [base]

                    def step(ins):
                        ins.then_inc(s_bn, 1)
                        n_bn[0] += 1
                        dve.wait_ge(s_bn, n_bn[0])

                    gam, bet, bias = (cols_in[:, 3 * l + c, :] for c in range(3))
                    T = lambda c: bn_tmp[:, c, :]
                    dve.wait_ge(s_bn_pe, l + 1)
                    step(dve.tensor_scalar(T(0), ps_m[0][:, 0:2], 1.0 / N, None, ALU.mult))
                    step(dve.tensor_scalar(T(1), ps_m[0][:, 2:4], 1.0 / N, None, ALU.mult))
                    step(dve.tensor_tensor(T(2), T(0), T(0), ALU.mult))
                    step(dve.tensor_tensor(T(3), T(1), T(2), ALU.subtract))
                    step(dve.tensor_scalar(T(4), T(3), 0.0, None, ALU.max))
                    step(dve.tensor_tensor(T(6), T(0), bias, ALU.add))
                    dve.wait_ge(s_bn_sqrt, l + 1)
                    step(dve.reciprocal(T(7), T(5)))
                    step(dve.tensor_tensor(scale_c[:, l, :], T(7), gam, ALU.mult))
                    step(dve.tensor_tensor(T(8), bias, T(6), ALU.subtract))
                    step(dve.tensor_tensor(T(9), T(8), scale_c[:, l, :], ALU.mult))
                    step(dve.memset(acc_z[:, :], 0.0))
                    step(dve.memset(acc_sq[:, :], 0.0))
                    dve.tensor_tensor(shift_c[:, l, :], T(9), bet, ALU.add).then_inc(s_bn_ready, 1)



_INS = ['x', 'src', 'dst', 'L0_gnn_Wl0', 'L0_gnn_bl0', 'L0_gnn_Wr0', 'L0_gnn_gamma0', 'L0_gnn_beta0', 'L0_gnn_Wl1',
        'L0_gnn_bl1', 'L0_gnn_Wr1', 'L0_gnn_gamma1', 'L0_gnn_beta1', 'L0_gnn_Wl2', 'L0_gnn_bl2', 'L0_gnn_Wr2']


def kernel(**inputs):
    import numpy as _np
    import concourse.bacc as _bacc
    from concourse import mybir as _mybir
    from concourse.bass_utils import run_bass_kernel_spmd as _run

    nc = _bacc.Bacc("TRN2", target_bir_lowering=False, num_devices=1)
    arrays, args = {}, []
    for name in _INS:
        a = _np.ascontiguousarray(inputs[name])
        arrays[f"in_{name}"] = a
        args.append(nc.dram_tensor(f"in_{name}", a.shape, _mybir.dt.from_np(a.dtype), kind="ExternalInput").ap())
    args.append(nc.dram_tensor("out_dram", inputs["x"].shape, _mybir.dt.float32, kind="ExternalOutput").ap())
    gnn_kernel(nc, *args)
    r = _run(nc, [arrays], core_ids=[0])
    return r.results[0]["out_dram"]
```

```python
from contextlib import ExitStack

import concourse.bass as bass
from concourse import mybir

F32 = mybir.dt.float32
I32 = mybir.dt.int32
F32R = mybir.dt.float32r
ALU = mybir.AluOpType
ACT = mybir.ActivationFunctionType
AX_X = mybir.AxisListType.X

P = 128
EPS = 1e-5
PAD_DST = float(1 << 20)


def gnn_kernel(nc, x, src, dst, Wl0, bl0, Wr0, gamma0, beta0, Wl1, bl1, Wr1, gamma1, beta1, Wl2, bl2, Wr2, out):
    N, CIN = x.shape
    E = src.shape[0]
    HID = Wl0.shape[0]
    COUT = Wl2.shape[0]
    NODES = 2 * P
    BLOCKS = -(-N // NODES)
    TAIL_P = (N - (BLOCKS - 1) * NODES) // 2
    ROW = 2 * P
    PAIRS = -(-E // ROW)
    EPAD = PAIRS * ROW
    TILES = 2 * PAIRS
    GROUPS = -(-(BLOCKS + 1) // PAIRS)
    U = 6
    R = 3
    EVERY = -(-BLOCKS // PAIRS)
    BODY = EVERY * R
    AHEAD = 3
    LAST_ROW = E - (PAIRS - 1) * ROW
    LINE = ROW
    LINES = PAIRS
    assert BODY % U == 0 and EVERY % 2 == 0
    assert CIN == P and COUT == P and HID == 2 * P and N % 2 == 0 and PAIRS <= P
    assert GROUPS * PAIRS > BLOCKS

    K_IN = [CIN, HID, HID]
    K_OUT = [HID, HID, COUT]
    CH = [k // P for k in K_IN]

    z_dram = [nc.dram_tensor(f"z{n}", [N, HID], F32, kind="Internal").ap() for n in range(2)]
    y_dram = [nc.dram_tensor(f"y{n}", [EPAD + P, K_OUT[n] + 1], F32, kind="Internal").ap() for n in range(3)]
    dst_rows_dram = nc.dram_tensor("dst_rows", [PAIRS + 1, ROW], F32, kind="Internal").ap()
    unsorted_dram = nc.dram_tensor("unsorted", [EPAD], F32, kind="Internal").ap()
    sorted_dram = nc.dram_tensor("sorted", [EPAD, 2], F32, kind="Internal").ap()
    start_dram = nc.dram_tensor("starts", [PAIRS, GROUPS], I32, kind="Internal").ap()

    with ExitStack() as ctx:
        def sb(name, shape, dt=F32):
            return ctx.enter_context(nc.sbuf_tensor(name, shape, dt))

        def sem(name):
            return ctx.enter_context(nc.semaphore(name))

        def sems(name, n):
            return [sem(f"{name}{i}") for i in range(n)]

        ps_t = [ctx.enter_context(nc.psum_tensor(f"ps_t{i}", [P, 512], F32)) for i in range(R)]
        ps_z = [ctx.enter_context(nc.psum_tensor(f"ps_z{i}", [P, 512], F32)) for i in range(R)]
        ps_m = [ctx.enter_context(nc.psum_tensor(f"ps_m{i}", [P, 512], F32)) for i in range(2)]

        ident = sb("ident", [P, P])
        ones = sb("ones", [P, P])
        node_of_col = sb("node_of_col", [P, 2, P])
        eps_col = sb("eps_col", [P, 1])
        block_base = sb("block_base", [P, BLOCKS])
        w_raw = sb("w_raw", [P, 6, 2, HID])
        wT = sb("wT", [P, 6, 2, HID])
        cols_in = sb("cols_in", [P, 6, 2])
        bias2 = sb("bias2", [P, 2, COUT])
        scale_c = sb("scale_c", [P, 2, 2])
        shift_c = sb("shift_c", [P, 2, 2])
        bn_tmp = sb("bn_tmp", [P, 10, 2])

        src_i = sb("src_i", [P, ROW], I32)
        dst_i = sb("dst_i", [P, ROW], I32)
        src_f = sb("src_f", [P, ROW])
        dst_f = sb("dst_f", [P, ROW])
        dst_prev = sb("dst_prev", [P, ROW])
        dst_next = sb("dst_next", [P, ROW])
        edge_no = sb("edge_no", [P, ROW])
        next_i = sb("next_i", [P, ROW], I32)
        next_f = sb("next_f", [P, ROW])
        descents = sb("descents", [P, 1])
        unsorted = sb("unsorted_flag", [1, 1], I32)
        line = sb("line", [P, LINE])
        line_no = sb("line_no", [P, LINE])
        earlier = sb("earlier", [P, LINE])
        same = sb("same", [P, LINE])
        line_base = sb("line_base", [P, 1])
        edge_col = sb("edge_col", [P, TILES])
        pair_col = sb("pair_col", [P, TILES, 2])
        rank = sb("rank", [P, TILES])
        rank_part = sb("rank_part", [P, 2])
        rank_i = sb("rank_i", [P, TILES], I32)
        rank_now = sb("rank_now", [P, 1], I32)
        pair_now = sb("pair_now", [P, 2])
        sorted_rows = sb("sorted_rows", [P, ROW, 2])
        run_a = sb("run_a", [P, ROW])
        run_b = sb("run_b", [P, ROW])
        run_first = sb("run_first", [P, ROW])
        run_last = sb("run_last", [P, ROW])
        inv_cnt = sb("inv_cnt", [P, ROW])
        row_ends = sb("row_ends", [P, 2])
        row_line = sb("row_line", [1, 4, P])
        carry = sb("carry", [P, 2])
        diag = sb("diag", [P, P])
        thresholds = sb("thresholds", [P, GROUPS])
        coarse = sb("coarse", [P, GROUPS])
        coarse_i = sb("coarse_i", [P, GROUPS], I32)
        found_row = sb("found_row", [P, GROUPS, ROW])
        fine = sb("fine", [P, GROUPS])
        scratch = sb("scratch", [P, ROW])
        start_i = sb("start_i", [P, GROUPS], I32)
        start_line = sb("start_line", [1, PAIRS * GROUPS], I32)
        start_f = sb("start_f", [1, PAIRS * GROUPS])
        more_f = sb("more_f", [1, BLOCKS])
        more_i = sb("more_i", [1, BLOCKS], I32)
        more_r = sb("more_r", [1, BLOCKS])
        stored_before = sb("stored_before", [1, BLOCKS + EVERY])
        late = sb("late", [1, BLOCKS])
        before_f = sb("before_f", [1, BLOCKS])
        before_i = sb("before_i", [1, BLOCKS], I32)
        line_of_ones = sb("line_of_ones", [1, BLOCKS])
        any_f = sb("any_f", [1, 1])
        apart_flag = sb("apart_flag", [1, 1], I32)
        win_more = sb("win_more", [P, HID + 1])
        sel_more = sb("sel_more", [P, 2, P])
        src_col = sb("src_col", [P, TILES], I32)
        dst_col = sb("dst_col", [P, TILES])
        inv_col = sb("inv_col", [P, TILES])
        idx_ring = sb("idx_ring", [P, R, 2], I32)
        y_pad = sb("y_pad", [P, HID + 1])

        rows_in = sb("rows_in", [P, U, 2 * HID])
        edge_rows = sb("edge_rows", [P, R, 2 * HID])
        x_in = sb("x_in", [P, U, 2 * CIN])
        win = sb("win", [P, U, HID + 1])
        class Norm:
            def __init__(self, kind, slots):
                self.slots = slots
                self.stats = sb(f"{kind}_ln_stats", [P, slots, 2, 6])
                self.mv = sb(f"{kind}_ln_mv", [P, slots, 2, 2])
                self.std = sb(f"{kind}_ln_std", [P, slots, 2])
                self.shift = sb(f"{kind}_ln_shift", [P, slots])
                self.rstd = sb(f"{kind}_ln_rstd", [P, slots, 2])

        norms = {"e": Norm("edge", R), "n": Norm("node", U)}
        h_rows_of = {k: sb(f"{k}_h_rows", [P, R, 2, CIN]) for k in "en"}
        hT_of = {k: sb(f"{k}_hT", [P, R, 2, 2, P]) for k in "en"}
        rows_of = {"e": edge_rows, "n": rows_in}
        turns_of = {"e": ps_m[0:1], "n": ps_t}
        products_of = {"e": ps_m[1:2], "n": ps_z}
        sel = sb("sel", [P, R, 2, P])
        sel_r = sb("sel_r", [P, R, 2, P], F32R)
        win_hi = sb("win_hi", [P, R, HID], F32R)
        win_lo = sb("win_lo", [P, R, HID], F32R)
        parts_of = {k: [sb(f"{k}_hT_{part}", [P, slots, 2, 2, P], F32R) for part in ("hi", "lo")] for k, slots in (("e", 1), ("n", R))}
        w_hi = sb("w_hi", [P, 2, 2, HID], F32R)
        w_lo = sb("w_lo", [P, 2, 2, HID], F32R)
        z_sb = sb("z_sb", [P, U, 2 * HID])
        z_sq = sb("z_sq", [P, R, 512])
        y_sb = sb("y_sb", [P, R, 2, HID + 1])
        acc_z = sb("acc_z", [P, 512])
        acc_sq = sb("acc_sq", [P, 512])
        t_sb = sb("t_sb", [P, U, 2, COUT])
        neg_max = sb("neg_max", [P, U, 2])
        exp_sum = sb("exp_sum", [P, U, 2])
        log_sum = sb("log_sum", [P, U, 2])
        soft_shift = sb("soft_shift", [P, U, 2])

        s_const = sem("s_const")
        s_params = sem("s_params")
        s_pool = sem("s_pool")
        s_wt = sem("s_wt")
        s_wc = sem("s_wc")
        s_edges = sem("s_edges")
        s_dstf = sem("s_dstf")
        s_shift = sem("s_shift")
        s_flag_dve = sem("s_flag_dve")
        s_hi = sem("s_hi")
        s_hT_hi = {k: sem(f"s_hT_hi_{k}") for k in "en"}
        s_w_parts = sem("s_w_parts")
        s_meta = sem("s_meta")
        s_meta_pe = sem("s_meta_pe")
        s_found = sem("s_found")
        s_start = sem("s_start")
        s_ypad = sem("s_ypad")
        s_bn_pe = sem("s_bn_pe")
        s_bn = sem("s_bn")
        s_bn_sqrt = sem("s_bn_sqrt")
        s_bn_ready = sem("s_bn_ready")

        def uses(count, slot, slots):
            return (count - slot + slots - 1) // slots

        class Ring:
            def __init__(self, layer, count):
                self.layer, self.count = layer, count

            def landed(self, slot, turn):
                return (turn + 1 + self.layer * uses(self.count, slot, R)) * 32

            def window(self, slot, turn):
                return (turn + 1 + self.layer * uses(self.count, slot, U)) * 16

            def kept(self, slot, turn):
                return (turn + self.layer * uses(self.count, slot, R)) * 16

            def all_kept(self, slot):
                return self.kept(slot, uses(self.count, slot, R))

            def twos(self, two):
                count = (self.count + 1) // 2
                return uses(count, two, U // 2) + (self.count % 2 == 0 and two == (count - 1) % (U // 2))

            def two_moved(self, slot, turn, layer=None):
                return (turn + (self.layer if layer is None else layer) * self.twos(slot // 2)) * 16

            def here(self, i, slot, turn, layer=None):
                in_two_transfers = isinstance(i, int) and self.count % 2 == 0 and i >= self.count - 2
                return self.two_moved(slot, turn + 1 + in_two_transfers, layer)

            def all_moved(self, two):
                return (self.layer + 1) * self.twos(two) * 16

        dma_sems = {"e": (sems("e_loaded", R), sems("e_stored", R)),
                    "n": (sems("n_loaded", U // 2), sems("n_stored", U // 2))}
        window_sems = sems("n_window", U)
        edge, node = [], []
        for l in range(3):
            for kind, into in (("e", edge), ("n", node)):
                r = Ring(l, PAIRS if kind == "e" else BLOCKS)
                r.loaded, r.stored = dma_sems[kind]
                r.turns, r.products, r.rows_in = turns_of[kind], products_of[kind], rows_of[kind]
                r.norm, r.h_rows, r.hT_sb = norms[kind], h_rows_of[kind], hT_of[kind]
                r.hT_parts = parts_of[kind]
                if l == 1:
                    r.parts = sem(f"{kind}1_parts")
                r.slots = R if kind == "e" else U
                r.turned = sem(f"{kind}{l}_turned")
                r.hT = sem(f"{kind}{l}_hT")
                r.prod = sem(f"{kind}{l}_prod")
                r.out = sem(f"{kind}{l}_out")
                if l == 0:
                    r.stat = sem(f"{kind}{l}_stat")
                    r.std = sem(f"{kind}{l}_std")
                    r.rstd = sem(f"{kind}{l}_rstd")
                    r.shift = sem(f"{kind}{l}_shift")
                    r.rows = sem(f"{kind}{l}_rows")
                    r.rows_act = sem(f"{kind}{l}_rows_act")
                if kind == "e":
                    r.idx = sem(f"e{l}_idx")
                else:
                    r.win = window_sems
                    r.sel = sem(f"n{l}_sel")
                    r.more_loaded = sem(f"n{l}_more_loaded")
                    r.more_sel = sem(f"n{l}_more_sel")
                    r.more_done = sem(f"n{l}_more_done")
                    if l < 2:
                        r.acc = sem(f"n{l}_acc")
                        r.acc_z = sem(f"n{l}_acc_z")
                    else:
                        r.top = sem("n2_top")
                        r.x = sems("n2_x", U // 2)
                        r.log = sem("n2_log")
                into.append(r)
        s_chain = sem("s_chain")

        s_ln = {k: sem(f"s_ln_{k}") for k in "en"}
        s_flag_pe = sem("s_flag_pe")
        s_flag = sem("s_flag")
        s_more = sem("s_more")
        q_out = sem("q_out")
        q_cols = sem("q_cols")
        q_line = sem("q_line")
        q_chain = sem("q_chain")
        q_used = sem("q_used")
        q_rank = sem("q_rank")
        q_now = sem("q_now")
        q_put = sem("q_put")
        q_back = sem("q_back")
        s_gate = sem("s_gate")
        s_gate_pool = sem("s_gate_pool")
        s_gate_sp = sem("s_gate_sp")
        s_exp = sem("s_exp")
        s_logit = sem("s_logit")
        s_shift2 = sem("s_shift2")
        for l in range(2):
            node[l].sq = sem(f"n{l}_sq")

        S_CONST = 17
        META_SORTED = 3
        META_ENDS = 10
        META_DIAG = 11
        META_LINE = 15
        META_COARSE = 18
        META_INV = 25
        META_COLS = 26
        META_START = 27
        MORE_READY = 10
        WINDOW = [6, 5, 8]
        STORE = [AHEAD * EVERY + w + 2 for w in WINDOW]
        SPLIT = [False, True, False]

        def is_unsorted(eng):
            eng.wait_ge(s_flag, 1)
            return eng.value_load(unsorted[0:1, 0:1], min_val=0, max_val=EPAD)

        def runs_apart(eng):
            eng.wait_ge(s_more, MORE_READY)
            return eng.value_load(apart_flag[0:1, 0:1], min_val=0, max_val=TILES + BLOCKS)

        def more_of(eng, i):
            n = eng.value_load(more_i[0:1, bass.ds(i, 1)], min_val=0, max_val=TILES)
            before = eng.value_load(before_i[0:1, bass.ds(i, 1)], min_val=0, max_val=TILES)
            return n, before

        def for_each_more(eng, i, body):
            n, before = more_of(eng, i)
            with eng.If(n > 0):
                with eng.Fori(0, n) as w:
                    body(w, before + w)

        class Stage:
            def __init__(self, offset, fn, count, slots, per=1, two_blocks=False):
                self.offset, self.fn, self.count, self.slots, self.per, self.two = offset, fn, count, slots, per, two_blocks

            def run(self, n, k=None, body=0):
                n += self.offset
                i = n // self.per
                if n % self.per or (self.two and i % 2) or (k is None and not 0 <= i < self.count):
                    return
                slot, turn = i % self.slots, i // self.slots
                if k is not None:
                    i, turn = i + k * (body // self.per), turn + k * (body // self.per // self.slots)
                self.fn(i, slot, turn, slot % R, turn * (self.slots // R) + slot // R)

        def blocks(offset, fn):
            return Stage(offset, fn, BLOCKS, U)

        def two(offset, fn):
            return Stage(offset, fn, BLOCKS, U, two_blocks=True)

        def pairs(offset, fn, per=1):
            return Stage(offset, fn, PAIRS, R, per)

        def pipeline(eng, stages, body=U):
            first = -max(s.offset for s in stages)
            last = max((s.count - 1) * s.per - s.offset for s in stages)
            full = min(((s.count - 3) * s.per - s.offset - (body - 1)) // body for s in stages) + 1
            for n in range(first, min(body, last + 1)):
                for s in stages:
                    s.run(n)
            if full > 1:
                with eng.Fori(1, full) as k:
                    for n in range(body):
                        for s in stages:
                            s.run(n, k, body)
            for n in range(max(full, 1) * body, last + 1):
                for s in stages:
                    s.run(n)

        def passes(eng, apart, edge_stages, node_stages, between=None):
            with eng.If(apart > 0):
                if edge_stages:
                    pipeline(eng, [pairs(alone, fn) for alone, _, fn in edge_stages if alone is not None])
                if between:
                    between()
                pipeline(eng, node_stages(True))
            with eng.Else():
                pipeline(eng, [pairs(o, fn, EVERY) for _, o, fn in edge_stages] + node_stages(False), BODY)

        def free(eng, s, value):
            if isinstance(value, int) and value <= 0:
                return
            eng.wait_ge(s, value)

        def after(eng, s, i, lag):
            if isinstance(i, int):
                if i >= lag:
                    eng.wait_ge(s, i - lag + 1)
                return
            eng.wait_ge(s, i + (1 - lag))

        def rows_here(r, kind, i, u, t):
            return (r.loaded[u], r.landed(u, t)) if kind == "e" else (r.loaded[u // 2], r.here(i, u, t))

        block = ctx.enter_context(nc.Block())

        def filled(i):
            return TAIL_P if isinstance(i, int) and i == BLOCKS - 1 else P

        W_ALL = [Wl0, Wr0, Wl1, Wr1, Wl2, Wr2]

        def y_rows(l, i):
            return y_dram[l][bass.ds(i * ROW, ROW), :].rearrange("(a p) f -> p a f", a=2)

        def two_blocks(eng, dram, sbuf, width, i, u, s, store=False):
            if isinstance(i, int) and i + 1 >= BLOCKS - 1:
                for b in range(i, BLOCKS):
                    q = filled(b)
                    there = dram[b * NODES:b * NODES + 2 * q, :].rearrange("(p j) f -> p (j f)", j=2)
                    here = sbuf[0:q, u + b - i, 0:2 * width]
                    eng.dma_start(*((there, here) if store else (here, there))).then_inc(s, 16)
                return
            there = dram[bass.ds(i * NODES, 2 * NODES), :].rearrange("(b p j) f -> p b (j f)", b=2, j=2)
            here = sbuf[:, u:u + 2, 0:2 * width]
            eng.dma_start(*((there, here) if store else (here, there))).then_inc(s, 16)

        @block.sync
        def _(sp):
            sp.wait_ge(s_const, 3)
            for a, t in ((src, src_i), (dst, dst_i)):
                sp.dma_start(t[0:PAIRS - 1, :], a[0:(PAIRS - 1) * ROW].rearrange("(r c) -> r c", c=ROW)).then_inc(s_edges, 16)
                sp.dma_start(t[PAIRS - 1:PAIRS, 0:LAST_ROW], a[(PAIRS - 1) * ROW:E].rearrange("(r c) -> r c", r=1)).then_inc(s_edges, 16)
            sp.dma_start(next_i[0:PAIRS - 1, :], dst[1:(PAIRS - 1) * ROW + 1].rearrange("(r c) -> r c", c=ROW)).then_inc(s_edges, 16)
            sp.dma_start(next_i[PAIRS - 1:PAIRS, 0:LAST_ROW - 1], dst[(PAIRS - 1) * ROW + 1:E].rearrange("(r c) -> r c", r=1)).then_inc(s_edges, 16)
            for m, w in enumerate(W_ALL):
                o, k = w.shape
                sp.dma_start(w_raw[:, m, 0:o // P, 0:k], w.rearrange("(c p) k -> p c k", p=P)).then_inc(s_params, 16)
            with nc.allow_non_contiguous_dma(reason="a few hundred values"):
                for m, v in enumerate((gamma0, beta0, bl0, gamma1, beta1, bl1)):
                    sp.dma_start(cols_in[:, m, :], v.rearrange("(c p) -> p c", p=P)).then_inc(s_params, 16)
            for j in range(2):
                sp.dma_start(bias2[:, j, :], bl2.rearrange("(a f) -> a f", a=1).to_broadcast([P, COUT])).then_inc(s_params, 16)
            flag = is_unsorted(sp)
            with sp.If(flag > 0):
                sp.dma_start(unsorted_dram.rearrange("(r c) -> r c", c=ROW), dst_f[0:PAIRS, :]).then_inc(q_out, 16)
                sp.wait_ge(q_out, 16)
                with sp.Fori(0, LINES) as c:
                    sp.wait_ge(q_used, c + 1)
                    sp.dma_start(line[:, :], unsorted_dram[bass.ds(c * LINE, LINE)].rearrange("(a n) -> a n", a=1)
                                 .to_broadcast([P, LINE])).then_inc(q_line, 16)
                sp.wait_ge(q_put, 16 * TILES)
                sp.dma_start(sorted_rows[0:PAIRS, :, :], sorted_dram.rearrange("(r c) v -> r c v", c=ROW)).then_inc(q_back, 16)
            sp.wait_ge(s_meta, META_SORTED)
            sp.dma_start(dst_rows_dram[0:PAIRS, :], dst_f[0:PAIRS, :]).then_inc(s_dstf, 16)
            sp.wait_ge(s_const, 6)
            sp.dma_start(dst_rows_dram[PAIRS:PAIRS + 1, :], scratch[0:1, :]).then_inc(s_dstf, 16)
            sp.wait_ge(s_dstf, 32)
            flat = dst_rows_dram.rearrange("r c -> (r c)")
            sp.dma_start(dst_prev[1:PAIRS, :], flat[ROW - 1:EPAD - 1].rearrange("(r c) -> r c", c=ROW)).then_inc(s_shift, 16)
            sp.dma_start(dst_prev[0:1, 1:ROW], flat[0:ROW - 1].rearrange("(r c) -> r c", r=1)).then_inc(s_shift, 16)
            sp.dma_start(dst_next[0:PAIRS, :], flat[1:EPAD + 1].rearrange("(r c) -> r c", c=ROW)).then_inc(s_shift, 16)
            for l in range(3):
                sp.dma_start(y_dram[l][EPAD:EPAD + P, :], y_pad[:, HID - K_OUT[l]:HID + 1]).then_inc(s_ypad, 16)
            sp.wait_ge(s_meta, META_START)
            sp.dma_start(start_dram, start_i[0:PAIRS, :]).then_inc(s_start, 16)
            sp.wait_ge(s_start, 16)
            sp.dma_start(start_line[0:1, :], start_dram.rearrange("r g -> (r g)").rearrange("(a n) -> a n", a=1)).then_inc(s_start, 16)
            sp.wait_ge(s_start, 32)
            sp.wait_ge(s_ypad, 48)

            apart = runs_apart(sp)
            for l in range(3):
                e, n = edge[l], node[l]
                W = K_OUT[l]

                def store_messages(i, u, t, v, w):
                    sp.wait_ge(e.out, i + 1)
                    sp.dma_start(y_rows(l, i), y_sb[:, v, :, 0:W + 1]).then_inc(e.stored[v], 16)

                def messages_stored(i, u, t, v, w):
                    sp.wait_ge(e.stored[v], e.kept(v, w + 1))
                    sp.sem_inc(s_gate_sp, 1)

                def all_stored():
                    for v in range(R):
                        sp.wait_ge(e.stored[v], e.all_kept(v))

                def load_rows(i, u, t, v, w):
                    for s in (n.rows, n.rows_act) if l == 0 else (n.turned,):
                        after(sp, s, min(i + 1, BLOCKS - 1) if isinstance(i, int) else i + 1, U)
                    two_blocks(sp, x if l == 0 else z_dram[l - 1], rows_in, K_IN[l], i, u, n.loaded[u // 2])

                def load_window(i, u, t, v, w):
                    after(sp, n.prod, i, U)
                    start = sp.value_load(start_line[0:1, bass.ds(i, 1)], min_val=0, max_val=EPAD)
                    sp.dma_start(win[:, u, 0:W + 1], y_dram[l][bass.ds(start, P), :]).then_inc(n.win[u], 16)

                def store_blocks(i, u, t, v, w):
                    sp.wait_ge(n.out, min(i + 2, BLOCKS) if isinstance(i, int) else i + 2)
                    two_blocks(sp, z_dram[l] if l < 2 else out, z_sb, HID if l < 2 else COUT, i, u,
                               n.stored[u // 2], store=True)

                passes(sp, apart, [(0, STORE[l], store_messages), (None, AHEAD * EVERY + WINDOW[l], messages_stored)],
                       lambda with_more: [two((10, 8, 10)[l], load_rows), blocks(WINDOW[l], load_window), two(0, store_blocks)],
                       all_stored)
                for c in range(U // 2):
                    sp.wait_ge(n.stored[c], n.all_moved(c))


        @block.gpsimd
        def _(pool):
            pool.memset(src_i[:, :], 0).then_inc(s_const, 1)
            pool.memset(dst_i[:, :], int(PAD_DST)).then_inc(s_const, 1)
            pool.memset(next_i[:, :], int(PAD_DST)).then_inc(s_const, 1)
            pool.memset(scratch[:, :], PAD_DST).then_inc(s_const, 1)
            pool.memset(y_pad[:, :], -1.0).then_inc(s_const, 1)
            pool.memset(dst_prev[:, :], -1.0).then_inc(s_const, 1)
            pool.memset(ident[:, :], 0.0).then_inc(s_pool, 1)
            pool.memset(ones[:, :], 1.0).then_inc(s_const, 1)
            pool.memset(line_of_ones[:, :], 1.0).then_inc(s_const, 1)
            pool.iota(line_no[:, :], pattern=[[1, LINE]], base=0, channel_multiplier=0,
                      allow_small_or_imprecise_dtypes=True).then_inc(s_const, 1)
            pool.iota(edge_col[:, :], pattern=[[P, TILES]], base=0, channel_multiplier=1,
                      allow_small_or_imprecise_dtypes=True).then_inc(s_const, 1)
            pool.wait_ge(s_pool, 1)
            pool.affine_select(out=ident[:, :], in_=ident[:, :], compare_op=ALU.not_equal, fill=1.0,
                               base=0, pattern=[[-1, P]], channel_multiplier=1).then_inc(s_const, 1)
            pool.iota(edge_no[:, :], pattern=[[1, ROW]], base=0, channel_multiplier=ROW,
                      allow_small_or_imprecise_dtypes=True).then_inc(s_const, 1)
            pool.iota(thresholds[:, :], pattern=[[NODES, GROUPS]], base=0, channel_multiplier=GROUPS * NODES,
                      allow_small_or_imprecise_dtypes=True).then_inc(s_const, 1)
            pool.iota(node_of_col[:, :, :], pattern=[[1, 2], [2, P]], base=0, channel_multiplier=0,
                      allow_small_or_imprecise_dtypes=True).then_inc(s_const, 1)
            pool.iota(block_base[:, :], pattern=[[NODES, BLOCKS]], base=0, channel_multiplier=0,
                      allow_small_or_imprecise_dtypes=True).then_inc(s_const, 1)
            pool.iota(stored_before[0:1, 0:-(-BLOCKS // EVERY) * EVERY], pattern=[[ROW, -(-BLOCKS // EVERY)], [0, EVERY]],
                      base=(AHEAD + 1) * ROW - P, channel_multiplier=0, allow_small_or_imprecise_dtypes=True).then_inc(s_const, 1)
            pool.memset(eps_col[:, :], EPS).then_inc(s_const, 1)
            flag = is_unsorted(pool)
            with pool.If(flag > 0):
                pool.wait_ge(q_rank, 1)
                with pool.Fori(0, TILES) as t:
                    pool.tensor_copy(rank_now[:, :], rank_i[:, bass.ds(t, 1)]).then_inc(q_now, 1)
                    pool.tensor_copy(pair_now[:, :], pair_col[:, bass.ds(t, 1), :].rearrange("p a v -> p (a v)")).then_inc(q_now, 1)
                    pool.wait_ge(q_now, t * 2 + 2)
                    pool.sem_inc(s_gate_pool, 1)
                    pool.indirect_dma_start(out=sorted_dram, out_offset=bass.IndirectOffsetOnAxis(ap=rank_now[:, 0:1], axis=0),
                                            in_=pair_now[:, :], in_offset=None, bounds_check=EPAD - 1, oob_is_err=False).then_inc(q_put, 16)
                    pool.wait_ge(q_put, t * 16 + 16)
                    pool.sem_inc(s_gate_pool, 1)
            pool.wait_ge(s_meta, META_COARSE)
            pool.wait_ge(s_dstf, 32)
            for g in range(GROUPS):
                pool.indirect_dma_start(out=found_row[0:PAIRS, g, :], out_offset=None, in_=dst_rows_dram,
                                        in_offset=bass.IndirectOffsetOnAxis(ap=coarse_i[0:PAIRS, g:g + 1], axis=0),
                                        bounds_check=PAIRS, oob_is_err=False).then_inc(s_found, 16)
            pool.wait_ge(s_meta, META_COLS)
            apart = runs_apart(pool)
            for l in range(3):
                e = edge[l]
                if l > 0:
                    for c in range(U // 2):
                        pool.wait_ge(node[l - 1].stored[c], node[l - 1].all_moved(c))
                source = x if l == 0 else z_dram[l - 1]

                def gather(i, u, t, v, w):
                    for s in (e.rows, e.rows_act) if l == 0 else (e.turned,):
                        after(pool, s, i, R)
                    pool.sem_inc(s_gate_pool, 1)
                    pool.tensor_copy(idx_ring[:, u, :], src_col[:, bass.ds(i * 2, 2)]).then_inc(e.idx, 1)
                    pool.wait_ge(e.idx, i + 1)
                    pool.sem_inc(s_gate_pool, 1)
                    for a in range(2):
                        pool.indirect_dma_start(out=edge_rows[:, u, a * K_IN[l]:(a + 1) * K_IN[l]], out_offset=None, in_=source,
                                                in_offset=bass.IndirectOffsetOnAxis(ap=idx_ring[:, u, a:a + 1], axis=0),
                                                bounds_check=N - 1, oob_is_err=False).then_inc(e.loaded[u], 16)

                n = node[l]
                W = K_OUT[l]

                def pool_stages(with_more):
                    def load_more(i, u, t, v, w):
                        def window(m, k):
                            pool.wait_ge(n.more_done, k + 1)
                            pool.sem_inc(s_gate_pool, 1)
                            start = pool.value_load(start_line[0:1, bass.ds(i, 1)], min_val=0, max_val=EPAD)
                            first = nc.s_assert_within(start + (m + 1) * P, 0, EPAD, skip_runtime_bounds_check_because=
                                                       "the block's edges reach past it")
                            pool.dma_start(win_more[:, 0:W + 1], y_dram[l][bass.ds(first, P), :]).then_inc(n.more_loaded, 16)
                        for_each_more(pool, i, window)

                    def sum_z(i, u, t, v, w):
                        q = filled(i)
                        pool.wait_ge(n.out, i + 1)
                        after(pool, n.acc_z, i, 1)
                        pool.tensor_tensor(acc_z[0:q, :], acc_z[0:q, :], z_sb[0:q, u, :], ALU.add).then_inc(n.acc_z, 1)

                    def load_x(i, u, t, v, w):
                        after(pool, n.out, min(i + 1, BLOCKS - 1) if isinstance(i, int) else i + 1, U)
                        pool.sem_inc(s_gate_pool, 1)
                        two_blocks(pool, x, x_in, CIN, i, u, n.x[u // 2])

                    return [blocks(5, load_more)] * with_more + [blocks(0, sum_z) if l < 2 else two(5, load_x)]

                passes(pool, apart, [(0, STORE[l] + (21 if l == 0 else 11), gather)], pool_stages)


        @block.tensor
        def _(pe):
            pe.wait_ge(s_const, S_CONST)
            for l in range(3):
                pe.sem_inc(node[l].more_done, 1)
            pe.wait_ge(s_meta, 2)
            pe.matmul(ps_m[0][0:1, 0:1], ones[0:PAIRS, 0:1], descents[0:PAIRS, :], start=True, stop=True).then_inc(s_flag_pe, 1)
            flag = is_unsorted(pe)
            with pe.If(flag > 0):
                for c, t in enumerate((dst_f, src_f)):
                    for a in range(2):
                        mm = pe.transpose(ps_t[c][:, a * P:a * P + PAIRS], t[0:PAIRS, a * P:(a + 1) * P], ident[0:PAIRS, 0:PAIRS])
                mm.then_inc(q_cols, 1)
            pe.wait_ge(s_meta, META_ENDS)
            for c in range(2):
                mm = pe.transpose(ps_m[0][0:1, c * P:c * P + PAIRS], row_ends[0:PAIRS, c:c + 1], ident[0:PAIRS, 0:PAIRS])
            mm.then_inc(s_meta_pe, 1)
            pe.wait_ge(s_meta, META_DIAG)
            pe.matmul(ps_m[1][0:PAIRS, 0:PAIRS], ones[0:PAIRS, 0:PAIRS], diag[0:PAIRS, 0:PAIRS],
                      start=True, stop=True).then_inc(s_meta_pe, 1)
            pe.wait_ge(s_meta, META_LINE)
            for c in range(2):
                mm = pe.transpose(ps_m[0][0:PAIRS, 256 + c:257 + c], row_line[0:1, 2 + c, 0:PAIRS], ident[0:1, 0:1])
            mm.then_inc(s_meta_pe, 1)
            pe.wait_ge(s_meta, META_INV)
            for c, t in enumerate((src_f, dst_f, inv_cnt)):
                for a in range(2):
                    mm = pe.transpose(ps_t[c][:, a * P:a * P + PAIRS], t[0:PAIRS, a * P:(a + 1) * P], ident[0:PAIRS, 0:PAIRS])
            mm.then_inc(s_meta_pe, 1)
            pe.wait_ge(s_params, 16 * 14)
            g = 0
            for m, w in enumerate(W_ALL):
                o, k = w.shape
                for c in range(k // P):
                    if g >= R:
                        pe.wait_ge(s_wc, g - R + 1)
                    for h in range(o // P):
                        mm = pe.transpose(ps_z[g % R][:, h * P:(h + 1) * P], w_raw[:, m, h, c * P:(c + 1) * P], ident[:, :])
                    mm.then_inc(s_wt, 1)
                    g += 1
            pe.wait_ge(s_wc, g)
            pe.wait_ge(s_meta, META_COLS)
            apart = runs_apart(pe)
            for l in range(3):
                W = K_OUT[l]
                if l > 0:
                    pe.wait_ge(s_bn_ready, l)

                def stages(r, kind, with_more=False):
                    def turn(i, u, t, v, w):
                        q = filled(i) if kind == "n" else P
                        if l == 0:
                            pe.wait_ge(r.rows, i + 1)
                            pe.wait_ge(r.rows_act, i + 1)
                        else:
                            pe.wait_ge(*rows_here(r, kind, i, u, t))
                        ps = r.turns[v % len(r.turns)]
                        after(pe, r.hT, i, len(r.turns))
                        for c in range(CH[l]):
                            for j in range(2):
                                a = r.h_rows[0:q, v, j, :] if l == 0 else r.rows_in[0:q, u, (CH[l] * j + c) * P:(CH[l] * j + c + 1) * P]
                                mm = pe.transpose(ps[:, (2 * c + j) * P:(2 * c + j) * P + q], a, ident[0:q, 0:q])
                        mm.then_inc(r.turned, 1)

                    def product(i, u, t, v, w):
                        q = filled(i) if kind == "n" else P
                        if kind == "n":
                            pe.wait_ge(r.sel, i + 1)
                            pe.wait_ge(r.win[u], r.window(u, t))
                        ps = r.products[v % len(r.products)]
                        after(pe, r.out if kind == "e" else (r.sq if l < 2 else r.top), i, len(r.products))
                        if kind == "n" and SPLIT[l]:
                            for j in range(2):
                                for part in (win_hi, win_lo):
                                    pe.matmul(ps[0:q, j * W:(j + 1) * W], sel_r[:, v, j, 0:q], part[:, v, 0:W],
                                              start=(j == 0 and part is win_hi), stop=False, skip_group_check=True)
                        elif kind == "n":
                            for j in range(2):
                                pe.matmul(ps[0:q, j * W:(j + 1) * W], sel[:, v, j, 0:q], win[:, u, 0:W],
                                          start=(j == 0), stop=False, skip_group_check=True)

                        def window(m, k):
                            pe.wait_ge(r.more_sel, k + 1)
                            for j in range(2):
                                mm = pe.matmul(ps[0:q, j * W:(j + 1) * W], sel_more[:, j, 0:q], win_more[:, 0:W],
                                               start=False, stop=False, skip_group_check=True)
                            mm.then_inc(r.more_done, 1)

                        if with_more:
                            for_each_more(pe, i, window)
                        if SPLIT[l]:
                            pe.wait_ge(r.parts, i + 1)
                            hi, lo = r.hT_parts
                            side, p = int(kind == "n"), v % hi.shape[1]
                            for j in range(2):
                                for c in range(CH[l]):
                                    for h, wt in ((hi, w_hi), (lo, w_hi), (hi, w_lo)):
                                        mm = pe.matmul(ps[0:q, j * W:(j + 1) * W], h[:, p, c, j, 0:q], wt[:, side, c, 0:W],
                                                       start=(kind == "e" and j == 0 and c == 0 and h is hi and wt is w_hi),
                                                       stop=(j == 1 and c == CH[l] - 1 and wt is w_lo), skip_group_check=True)
                            mm.then_inc(r.prod, 1)
                            return
                        pe.wait_ge(r.hT, i + 1)
                        for j in range(2):
                            for c in range(CH[l]):
                                mm = pe.matmul(ps[0:q, j * W:(j + 1) * W], r.hT_sb[:, v, c, j, 0:q],
                                               wT[:, 2 * l + (kind == "n"), c, 0:W],
                                               start=(kind == "e" and j == 0 and c == 0), stop=(j == 1 and c == CH[l] - 1),
                                               skip_group_check=True)
                        mm.then_inc(r.prod, 1)

                    return turn, product

                def node_stages(with_more):
                    turn, product = stages(node[l], "n", with_more)
                    return [blocks((3, 3, 5)[l], turn), blocks((1, 1, 4)[l], product)]

                if SPLIT[l]:
                    pe.wait_ge(s_w_parts, 2)
                turn, product = stages(edge[l], "e")
                passes(pe, apart, [(2, STORE[l] + 7, turn), (1, STORE[l] + 2, product)], node_stages)
                if l < 2:
                    pe.wait_ge(node[l].acc, BLOCKS)
                    pe.wait_ge(node[l].acc_z, BLOCKS)
                    for s, acc in enumerate((acc_z, acc_sq)):
                        for c in range(2):
                            for j in range(2):
                                mm = pe.matmul(ps_m[0][:, 2 * s + c:2 * s + c + 1], acc[:, j * W + c * P:j * W + (c + 1) * P],
                                               ones[:, 0:1], start=(j == 0), stop=(j == 1), skip_group_check=True)
                    mm.then_inc(s_bn_pe, 1)


        @block.scalar
        def _(act):
            g = 0
            for m, w in enumerate(W_ALL):
                o, k = w.shape
                for c in range(k // P):
                    act.wait_ge(s_wt, g + 1)
                    act.activation(wT[:, m, c, 0:o], ps_z[g % R][:, 0:o], ACT.Copy).then_inc(s_wc, 1)
                    g += 1
            act.wait_ge(s_const, S_CONST)
            apart = runs_apart(act)

            for l in range(3):
                W = K_OUT[l]
                if l > 0:
                    act.wait_ge(s_bn_ready, l)
                act.preload_act_table_set("sqrt_and_others" if l < 2 else "natural_log_exp_and_others")

                def stages(r, kind):
                    def std(i, u, t, v, w):
                        q = filled(i) if kind == "n" else P
                        act.wait_ge(r.stat, i + 1)
                        after(act, r.rstd, i, r.slots)
                        act.activation(r.norm.std[0:q, u, :], r.norm.mv[0:q, u, :, 1], ACT.Sqrt, bias=eps_col[0:q, :]).then_inc(r.std, 1)

                    def norm(i, u, t, v, w):
                        q = filled(i) if kind == "n" else P
                        act.wait_ge(r.shift, i + 1)
                        act.wait_ge(*rows_here(r, kind, i, u, t))
                        after(act, r.turned, i, R)
                        act.activation(r.h_rows[0:q, v, 0, :], r.rows_in[0:q, u, 0:CIN], ACT.Relu,
                                       bias=r.norm.shift[0:q, u:u + 1], scale=r.norm.rstd[0:q, u, 0:1]).then_inc(r.rows_act, 1)

                    def copy_hT(i, u, t, v, w):
                        q = filled(i) if kind == "n" else P
                        act.wait_ge(r.turned, i + 1)
                        after(act, r.parts if SPLIT[l] else r.prod, i, R)
                        for c in range(CH[l]):
                            a = r.turns[v % len(r.turns)][:, 2 * c * P:2 * (c + 1) * P].rearrange("p (j n) -> p j n", j=2)[:, :, 0:q]
                            if l == 0:
                                ins = act.activation(r.hT_sb[:, v, c, :, 0:q], a, ACT.Relu)
                            else:
                                ins = act.activation(r.hT_sb[:, v, c, :, 0:q], a, ACT.Relu,
                                                     bias=shift_c[:, l - 1, c:c + 1], scale=scale_c[:, l - 1, c:c + 1])
                        ins.then_inc(r.hT, 1)

                    def messages(i, u, t, v, w):
                        act.wait_ge(r.prod, i + 1)
                        free(act, r.stored[v], r.kept(v, w))
                        act.activation(y_sb[:, v, :, W:W + 1], dst_col[:, bass.ds(i * 2, 2)].rearrange("p (a o) -> p a o", o=1), ACT.Copy)
                        for a in range(2):
                            ins = act.activation(y_sb[:, v, a, 0:W], r.products[v % len(r.products)][:, a * W:(a + 1) * W],
                                                 ACT.Copy, scale=inv_col[:, bass.ds(i * 2 + a, 1)])
                        ins.then_inc(r.out, 1)

                    def copy_z(i, u, t, v, w):
                        q = filled(i)
                        act.wait_ge(r.prod, i + 1)
                        free(act, r.stored[u // 2], r.two_moved(u, t))
                        after(act, r.acc_z, i, U)
                        act.activation(z_sb[0:q, u, :], ps_z[v][0:q, :], ACT.Copy).then_inc(r.out, 1)
                        after(act, r.acc, i, R)
                        act.activation(z_sq[0:q, v, :], ps_z[v][0:q, :], ACT.Square).then_inc(r.sq, 1)

                    def exponentials(i, u, t, v, w):
                        q = filled(i)
                        act.wait_ge(r.top, i + 1)
                        for j in range(2):
                            ins = act.activation(z_sq[0:q, v, j * COUT:(j + 1) * COUT], t_sb[0:q, u, j, :], ACT.Exp,
                                                 bias=neg_max[0:q, u, j:j + 1], accum_out=exp_sum[0:q, u, j:j + 1])
                        ins.then_inc(s_exp, 1)

                    def log(i, u, t, v, w):
                        q = filled(i)
                        act.wait_ge(s_exp, i + 1)
                        after(act, r.out, i, U)
                        act.activation(log_sum[0:q, u, :], exp_sum[0:q, u, :], ACT.Ln).then_inc(r.log, 1)

                    if l == 0:
                        if kind == "n":
                            return [(0, 0, copy_z), (6, 0, std), (4, 0, norm), (2, 0, copy_hT)]
                        return [(5, STORE[0] + 14, std), (3, STORE[0] + 11, norm), (2, STORE[0] + 6, copy_hT), (0, STORE[0] + 1, messages)]
                    if kind == "e":
                        return [(2, STORE[l] + 6, copy_hT)] + [(0, STORE[l] + 1, messages)] * (l == 1)
                    if l == 1:
                        return [(0, 0, copy_z), (3, 0, copy_hT)]
                    return [(1, 0, log), (5, 0, copy_hT), (2, 0, exponentials)]

                passes(act, apart, stages(edge[l], "e"),
                       lambda with_more: [blocks(offset, fn) for offset, _, fn in stages(node[l], "n")])
                if l < 2:
                    act.wait_ge(s_bn, 6 * (l + 1) + 6 * l)
                    act.activation(bn_tmp[:, 5, :], bn_tmp[:, 4, :], ACT.Sqrt, bias=eps_col[:, :]).then_inc(s_bn_sqrt, 1)


        @block.vector
        def _(dve):
            done = [0]

            def link(ins):
                ins.then_inc(s_meta, 1)
                done[0] += 1
                dve.wait_ge(s_meta, done[0])

            R_ = slice(0, PAIRS)
            dve.wait_ge(s_edges, 96)
            dve.tensor_copy(src_f[:, :], src_i[:, :])
            dve.tensor_copy(next_f[:, :], next_i[:, :])
            link(dve.tensor_copy(dst_f[:, :], dst_i[:, :]))
            dve.tensor_tensor(next_f[R_, :], next_f[R_, :], dst_f[R_, :], ALU.is_lt).then_inc(s_flag_dve, 1)
            dve.wait_ge(s_flag_dve, 1)
            link(dve.tensor_reduce(descents[R_, :], next_f[R_, :], AX_X, ALU.add))
            dve.wait_ge(s_flag_pe, 1)
            dve.tensor_copy(unsorted[0:1, 0:1], ps_m[0][0:1, 0:1]).then_inc(s_flag, 1)
            flag = is_unsorted(dve)
            with dve.If(flag > 0):
                dve.wait_ge(q_cols, 1)
                for c in range(2):
                    dve.tensor_copy(pair_col[:, :, c].rearrange("p (r a) -> p a r", a=2),
                                    ps_t[c][:, 0:2 * P].rearrange("p (a r) -> p a r", a=2)[:, :, R_])
                dve.memset(line_base[:, :], 0.0)
                dve.memset(rank[:, :], 0.0).then_inc(q_used, 1)
                dve.wait_ge(q_used, 1)
                with dve.Fori(0, LINES) as c:
                    dve.wait_ge(q_line, c * 16 + 16)
                    dve.sem_inc(s_gate, 1)
                    with dve.Fori(0, TILES) as t:
                        done_before = (c * TILES + t) * 5

                        def follow(ins, n):
                            ins.then_inc(q_chain, 1)
                            dve.wait_ge(q_chain, done_before + n)
                            dve.sem_inc(s_gate, 1)

                        follow(dve.tensor_scalar(earlier[:, :], line_no[:, :], line_base[:, 0:1], edge_col[:, bass.ds(t, 1)],
                                                 ALU.add, ALU.is_lt), 1)
                        follow(dve.scalar_tensor_tensor(out=same[:, :], in0=line[:, :],
                                                        scalar=pair_col[:, bass.ds(t, 1), 0:1].rearrange("p a v -> p (a v)"),
                                                        in1=earlier[:, :], op0=ALU.is_equal, op1=ALU.mult,
                                                        accum_out=rank_part[:, 0:1]), 2)
                        follow(dve.tensor_scalar(same[:, :], line[:, :], pair_col[:, bass.ds(t, 1), 0:1].rearrange("p a v -> p (a v)"),
                                                 None, ALU.is_lt, ALU.add, accum_out=rank_part[:, 1:2]), 3)
                        for n in range(2):
                            follow(dve.tensor_tensor(rank[:, bass.ds(t, 1)], rank[:, bass.ds(t, 1)], rank_part[:, n:n + 1], ALU.add), 4 + n)
                    dve.tensor_scalar(line_base[:, :], line_base[:, :], float(LINE), None, ALU.add).then_inc(q_used, 1)
                    dve.wait_ge(q_used, c + 2)
                dve.tensor_copy(rank_i[:, :], rank[:, :]).then_inc(q_rank, 1)
                dve.wait_ge(q_back, 16)
                dve.tensor_copy(dst_f[R_, :], sorted_rows[R_, :, 0])
                dve.tensor_copy(src_f[R_, :], sorted_rows[R_, :, 1])
            link(dve.memset(acc_sq[:, :], 0.0))
            dve.wait_ge(s_const, S_CONST)
            dve.wait_ge(s_shift, 48)
            link(dve.tensor_tensor(run_a[R_, :], dst_f[R_, :], dst_prev[R_, :], ALU.not_equal))
            link(dve.tensor_tensor(run_a[R_, :], run_a[R_, :], edge_no[R_, :], ALU.mult))
            link(dve.tensor_tensor(run_b[R_, :], dst_f[R_, :], dst_next[R_, :], ALU.is_equal))
            link(dve.scalar_tensor_tensor(out=run_b[R_, :], in0=run_b[R_, :], scalar=PAD_DST, in1=edge_no[R_, :],
                                          op0=ALU.mult, op1=ALU.add))
            link(dve.tensor_tensor_scan(run_first[R_, :], run_a[R_, :], run_a[R_, :], 0.0, ALU.max, ALU.max))
            link(dve.tensor_tensor_scan(run_last[R_, ::-1], run_b[R_, ::-1], run_b[R_, ::-1], 4 * PAD_DST, ALU.min, ALU.min))
            dve.tensor_copy(row_ends[R_, 0:1], run_first[R_, ROW - 1:ROW])
            link(dve.tensor_copy(row_ends[R_, 1:2], run_last[R_, 0:1]))
            link(dve.tensor_scalar(diag[R_, R_], ident[R_, R_], dst_f[R_, ROW - 1:ROW], None, ALU.mult))
            dve.wait_ge(s_meta_pe, 1)
            link(dve.tensor_copy(row_line[0:1, 0:2, R_], ps_m[0][0:1, 0:2 * P].rearrange("p (c n) -> p c n", c=2)[:, :, R_]))
            link(dve.memset(row_line[0:1, 2, 0:1], 0.0))
            dve.memset(row_line[0:1, 3, PAIRS - 1:PAIRS], 4 * PAD_DST)
            link(dve.tensor_tensor_scan(row_line[0:1, 2, 1:PAIRS], row_line[0:1, 0, 0:PAIRS - 1], row_line[0:1, 0, 0:PAIRS - 1],
                                        0.0, ALU.max, ALU.max))
            link(dve.tensor_tensor_scan(row_line[0:1, 3, PAIRS - 2::-1], row_line[0:1, 1, PAIRS - 1:0:-1],
                                        row_line[0:1, 1, PAIRS - 1:0:-1], 4 * PAD_DST, ALU.min, ALU.min))
            dve.wait_ge(s_meta_pe, 2)
            link(dve.tensor_copy(diag[R_, R_], ps_m[1][R_, R_]))
            for g in range(GROUPS):
                ins = dve.tensor_scalar(scratch[R_, R_], diag[R_, R_], thresholds[R_, g:g + 1], None, ALU.is_lt, ALU.add,
                                        accum_out=coarse[R_, g:g + 1])
                if g < GROUPS - 1:
                    ins.then_inc(s_chain, 1)
                    dve.wait_ge(s_chain, g + 1)
            link(ins)
            link(dve.tensor_copy(coarse_i[R_, :], coarse[R_, :]))
            dve.wait_ge(s_meta_pe, 3)
            link(dve.tensor_copy(carry[R_, :], ps_m[0][R_, 256:258]))
            link(dve.tensor_scalar(run_first[R_, :], run_first[R_, :], carry[R_, 0:1], None, ALU.max))
            link(dve.tensor_scalar(run_last[R_, :], run_last[R_, :], carry[R_, 1:2], None, ALU.min))
            link(dve.tensor_tensor(run_a[R_, :], run_last[R_, :], run_first[R_, :], ALU.subtract))
            link(dve.tensor_scalar(run_b[R_, :], run_a[R_, :], 1.0, 1.0, ALU.add, ALU.max))
            link(dve.reciprocal(inv_cnt[R_, :], run_b[R_, :]))
            link(dve.memset(acc_z[:, :], 0.0))
            dve.wait_ge(s_meta_pe, 4)
            for c, t in enumerate((src_col, dst_col, inv_col)):
                ins = dve.tensor_copy(t[:, :].rearrange("p (r a) -> p a r", a=2),
                                      ps_t[c][:, 0:2 * P].rearrange("p (a r) -> p a r", a=2)[:, :, R_])
            link(ins)
            dve.wait_ge(s_found, 16 * GROUPS)
            for g in range(GROUPS):
                dve.tensor_scalar(scratch[R_, :], found_row[R_, g, :], thresholds[R_, g:g + 1], None, ALU.is_lt, ALU.add,
                                  accum_out=fine[R_, g:g + 1]).then_inc(s_chain, 1)
                dve.wait_ge(s_chain, GROUPS + g)
            dve.scalar_tensor_tensor(out=start_i[R_, :], in0=coarse[R_, :], scalar=float(ROW), in1=fine[R_, :],
                                     op0=ALU.mult, op1=ALU.add).then_inc(s_meta, 1)
            dve.wait_ge(s_start, 32)

            def more_step(ins, n):
                ins.then_inc(s_more, 1)
                dve.wait_ge(s_more, n)

            more_step(dve.tensor_copy(start_f[:, :], start_line[:, :]), 1)
            more_step(dve.tensor_tensor(more_f[:, :], start_f[:, 1:BLOCKS + 1], start_f[:, 0:BLOCKS], ALU.subtract), 2)
            more_step(dve.tensor_scalar(more_r[:, :], more_f[:, :], 1.0 / P, -1.0 / P - 63.5 / P, ALU.mult, ALU.add), 3)
            more_step(dve.tensor_scalar(more_i[:, :], more_r[:, :], 0.0, None, ALU.max), 4)
            more_step(dve.tensor_copy(more_f[:, :], more_i[:, :]), 5)
            more_step(dve.tensor_tensor(late[:, :], start_f[:, 0:BLOCKS], stored_before[:, 0:BLOCKS], ALU.is_gt), 6)
            more_step(dve.tensor_tensor(late[:, :], late[:, :], more_f[:, :], ALU.add), 7)
            dve.tensor_reduce(any_f[:, :], late[:, :], AX_X, ALU.add)
            more_step(dve.tensor_tensor_scan(more_r[:, :], line_of_ones[:, :], more_f[:, :], 0.0, ALU.mult, ALU.add), 8)
            more_step(dve.tensor_copy(apart_flag[:, :], any_f[:, :]), 9)
            dve.tensor_tensor(before_i[:, :], more_r[:, :], more_f[:, :], ALU.subtract).then_inc(s_more, 1)
            dve.wait_ge(s_wc, 2 * sum(CH))
            dve.tensor_copy(w_hi[:, :, :, :], wT[:, 2:4, :, :]).then_inc(s_w_parts, 1)
            dve.wait_ge(s_w_parts, 1)
            dve.tensor_tensor(w_lo[:, :, :, :], wT[:, 2:4, :, :], w_hi[:, :, :, :].bitcast(F32), ALU.subtract).then_inc(s_w_parts, 1)
            apart = runs_apart(dve)
            for l in range(3):
                W = K_OUT[l]

                def stages(r, kind, with_more=False):
                    def stat(i, u, t, v, w):
                        q = filled(i) if kind == "n" else P
                        dve.wait_ge(*rows_here(r, kind, i, u, t))
                        for j in range(2):
                            dve.bn_stats(r.norm.stats[0:q, u, j, :], r.rows_in[0:q, u, j * CIN:(j + 1) * CIN]).then_inc(s_ln[kind], 1)

                    def aggregate(i, u, t, v, w):
                        q = filled(i) if kind == "n" else P
                        after(dve, r.std, i, r.slots)
                        dve.wait_ge(s_ln[kind], i * 2 + 2)
                        dve.sem_inc(s_gate, 1)
                        for j in range(2):
                            ins = dve.bn_aggr(r.norm.mv[0:q, u, j, :], r.norm.stats[0:q, u, j, :])
                        ins.then_inc(r.stat, 1)

                    def rstd(i, u, t, v, w):
                        q = filled(i) if kind == "n" else P
                        dve.wait_ge(r.std, i + 1)
                        after(dve, r.rows_act, i, r.slots)
                        dve.reciprocal(r.norm.rstd[0:q, u, :], r.norm.std[0:q, u, :]).then_inc(r.rstd, 1)

                    def norm(i, u, t, v, w):
                        q = filled(i) if kind == "n" else P
                        dve.wait_ge(r.rstd, i + 1)
                        dve.wait_ge(*rows_here(r, kind, i, u, t))
                        after(dve, r.turned, i, R)
                        dve.tensor_scalar(r.h_rows[0:q, v, 1, :], r.rows_in[0:q, u, CIN:2 * CIN], r.norm.mv[0:q, u, 1, 0:1],
                                          r.norm.rstd[0:q, u, 1:2], ALU.subtract, ALU.mult).then_inc(r.rows, 1)

                    def shift(i, u, t, v, w):
                        q = filled(i) if kind == "n" else P
                        dve.wait_ge(r.rstd, i + 1)
                        after(dve, r.rows_act, i, r.slots)
                        dve.scalar_tensor_tensor(out=r.norm.shift[0:q, u:u + 1], in0=r.norm.mv[0:q, u, 0, 0:1], scalar=-1.0,
                                                 in1=r.norm.rstd[0:q, u, 0:1], op0=ALU.mult, op1=ALU.mult).then_inc(r.shift, 1)

                    def messages(i, u, t, v, w):
                        dve.wait_ge(r.prod, i + 1)
                        free(dve, r.stored[v], r.kept(v, w))
                        dve.tensor_copy(y_sb[:, v, :, W:W + 1], dst_col[:, bass.ds(i * 2, 2)].rearrange("p (a o) -> p a o", o=1))
                        for a in range(2):
                            ins = dve.tensor_scalar(y_sb[:, v, a, 0:W], r.products[v % len(r.products)][:, a * W:(a + 1) * W],
                                                    inv_col[:, bass.ds(i * 2 + a, 1)], None, ALU.mult)
                        ins.then_inc(r.out, 1)

                    hi, lo = r.hT_parts

                    def upper(i, u, t, v, w):
                        q = filled(i) if kind == "n" else P
                        p = v % hi.shape[1]
                        dve.wait_ge(r.hT, i + 1)
                        after(dve, r.prod, i, hi.shape[1])
                        dve.tensor_copy(hi[:, p, :, :, 0:q], r.hT_sb[:, v, :, :, 0:q]).then_inc(s_hT_hi[kind], 1)

                    def lower(i, u, t, v, w):
                        q = filled(i) if kind == "n" else P
                        p = v % hi.shape[1]
                        dve.wait_ge(s_hT_hi[kind], i + 1)
                        dve.tensor_tensor(lo[:, p, :, :, 0:q], r.hT_sb[:, v, :, :, 0:q], hi[:, p, :, :, 0:q].bitcast(F32),
                                          ALU.subtract).then_inc(r.parts, 1)

                    def select(i, u, t, v, w):
                        dve.wait_ge(r.win[u], r.window(u, t))
                        after(dve, r.prod, i, R)
                        if SPLIT[l]:
                            dve.tensor_copy(win_hi[:, v, :], win[:, u, 0:W]).then_inc(s_hi, 1)
                        ins = dve.tensor_scalar((sel_r if SPLIT[l] else sel)[:, v, :, :], node_of_col[:, :, :],
                                                block_base[:, bass.ds(i, 1)], win[:, u, W:W + 1], ALU.add, ALU.is_equal)
                        if SPLIT[l]:
                            dve.wait_ge(s_hi, i + 1)
                            ins = dve.tensor_tensor(win_lo[:, v, :], win[:, u, 0:W], win_hi[:, v, :].bitcast(F32), ALU.subtract)
                        ins.then_inc(r.sel, 1)

                    def select_more(i, u, t, v, w):
                        def window(m, k):
                            dve.wait_ge(r.more_loaded, k * 16 + 16)
                            dve.sem_inc(s_gate, 1)
                            dve.tensor_scalar(sel_more[:, :, :], node_of_col[:, :, :], block_base[:, bass.ds(i, 1)],
                                              win_more[:, W:W + 1], ALU.add, ALU.is_equal).then_inc(r.more_sel, 1)

                        for_each_more(dve, i, window)

                    def sums(i, u, t, v, w):
                        q = filled(i)
                        dve.wait_ge(r.sq, i + 1)
                        after(dve, r.acc, i, 1)
                        dve.tensor_tensor(acc_sq[0:q, :], acc_sq[0:q, :], z_sq[0:q, v, :], ALU.add).then_inc(r.acc, 1)

                    def logits(i, u, t, v, w):
                        q = filled(i)
                        dve.wait_ge(r.prod, i + 1)
                        after(dve, r.log, i, U)
                        after(dve, r.out, i, U)
                        dve.tensor_tensor(t_sb[0:q, u, :, :], ps_z[v][0:q, 0:2 * COUT].rearrange("p (j f) -> p j f", j=2),
                                          bias2[0:q, :, :], ALU.add).then_inc(s_logit, 1)

                    def top(i, u, t, v, w):
                        q = filled(i)
                        dve.wait_ge(s_logit, i + 1)
                        dve.tensor_reduce(neg_max[0:q, u, :], t_sb[0:q, u, :, :], AX_X, ALU.max, negate=True).then_inc(r.top, 1)

                    def soft_shifts(i, u, t, v, w):
                        q = filled(i)
                        dve.wait_ge(r.log, i + 1)
                        after(dve, r.out, i, U)
                        dve.tensor_tensor(soft_shift[0:q, u, :], neg_max[0:q, u, :], log_sum[0:q, u, :], ALU.subtract).then_inc(s_shift2, 1)

                    def final(i, u, t, v, w):
                        q = filled(i)
                        dve.wait_ge(r.x[u // 2], r.here(i, u, t, 0))
                        free(dve, r.stored[u // 2], r.two_moved(u, t))
                        dve.wait_ge(s_shift2, i + 1)
                        for j in range(2):
                            ins = dve.scalar_tensor_tensor(out=z_sb[0:q, u, j * COUT:(j + 1) * COUT], in0=t_sb[0:q, u, j, :],
                                                           scalar=soft_shift[0:q, u, j:j + 1], in1=x_in[0:q, u, j * CIN:(j + 1) * CIN],
                                                           op0=ALU.add, op1=ALU.add)
                        ins.then_inc(r.out, 1)

                    if kind == "e":
                        return [[(3, STORE[0] + 11, norm), (6, STORE[0] + 17, stat), (6, STORE[0] + 15, aggregate), (4, STORE[0] + 12, rstd), (4, STORE[0] + 12, shift)],
                                [(1, STORE[1] + 4, upper), (1, STORE[1] + 3, lower)],
                                [(0, STORE[l] + 1, messages)]][l]
                    further = [blocks((1, 1, 4)[l], select_more)] * with_more
                    if l == 0:
                        return ([blocks(4, norm), blocks(7, stat), blocks(3, select), blocks(7, aggregate), blocks(5, rstd)]
                                + further + [blocks(0, sums), blocks(5, shift)])
                    if l == 1:
                        return [blocks(2, upper), blocks(2, select), blocks(2, lower)] + further + [blocks(0, sums)]
                    return ([blocks(5, select)] + further
                            + [blocks(0, soft_shifts), blocks(3, logits), blocks(0, final), blocks(3, top)])

                passes(dve, apart, stages(edge[l], "e"), lambda with_more: stages(node[l], "n", with_more))
                if l < 2:
                    base = 12 * l
                    n_bn = [base]

                    def step(ins):
                        ins.then_inc(s_bn, 1)
                        n_bn[0] += 1
                        dve.wait_ge(s_bn, n_bn[0])

                    gam, bet, bias = (cols_in[:, 3 * l + c, :] for c in range(3))
                    T = lambda c: bn_tmp[:, c, :]
                    dve.wait_ge(s_bn_pe, l + 1)
                    step(dve.tensor_scalar(T(0), ps_m[0][:, 0:2], 1.0 / N, None, ALU.mult))
                    step(dve.tensor_scalar(T(1), ps_m[0][:, 2:4], 1.0 / N, None, ALU.mult))
                    step(dve.tensor_tensor(T(2), T(0), T(0), ALU.mult))
                    step(dve.tensor_tensor(T(3), T(1), T(2), ALU.subtract))
                    step(dve.tensor_scalar(T(4), T(3), 0.0, None, ALU.max))
                    step(dve.tensor_tensor(T(6), T(0), bias, ALU.add))
                    dve.wait_ge(s_bn_sqrt, l + 1)
                    step(dve.reciprocal(T(7), T(5)))
                    step(dve.tensor_tensor(scale_c[:, l, :], T(7), gam, ALU.mult))
                    step(dve.tensor_tensor(T(8), bias, T(6), ALU.subtract))
                    step(dve.tensor_tensor(T(9), T(8), scale_c[:, l, :], ALU.mult))
                    step(dve.memset(acc_z[:, :], 0.0))
                    step(dve.memset(acc_sq[:, :], 0.0))
                    dve.tensor_tensor(shift_c[:, l, :], T(9), bet, ALU.add).then_inc(s_bn_ready, 1)



_INS = ['x', 'src', 'dst', 'L0_gnn_Wl0', 'L0_gnn_bl0', 'L0_gnn_Wr0', 'L0_gnn_gamma0', 'L0_gnn_beta0', 'L0_gnn_Wl1',
        'L0_gnn_bl1', 'L0_gnn_Wr1', 'L0_gnn_gamma1', 'L0_gnn_beta1', 'L0_gnn_Wl2', 'L0_gnn_bl2', 'L0_gnn_Wr2']


def kernel(**inputs):
    import numpy as _np
    import concourse.bacc as _bacc
    from concourse import mybir as _mybir
    from concourse.bass_utils import run_bass_kernel_spmd as _run

    nc = _bacc.Bacc("TRN2", target_bir_lowering=False, num_devices=1)
    arrays, args = {}, []
    for name in _INS:
        a = _np.ascontiguousarray(inputs[name])
        arrays[f"in_{name}"] = a
        args.append(nc.dram_tensor(f"in_{name}", a.shape, _mybir.dt.from_np(a.dtype), kind="ExternalInput").ap())
    args.append(nc.dram_tensor("out_dram", inputs["x"].shape, _mybir.dt.float32, kind="ExternalOutput").ap())
    gnn_kernel(nc, *args)
    r = _run(nc, [arrays], core_ids=[0])
    return r.results[0]["out_dram"]
```
